# Optimizing a Trainium2 kernel written in Bass

```python
import numpy as np
import jax
import jax.numpy as jnp

def _softmax(x, axis=-1):
    return jax.nn.softmax(x, axis=axis)

def _gelu(x):
    return jax.nn.gelu(x, approximate=True)

def _silu(x):
    return jax.nn.silu(x)

def _sigmoid(x):
    return jax.nn.sigmoid(x)

def _layernorm(x, axis=-1, eps=1e-05):
    m = jnp.mean(x, axis=axis, keepdims=True)
    v = jnp.var(x, axis=axis, keepdims=True)
    return (x - m) / jnp.sqrt(v + eps)

def _scatter_add(tgt, idx, src, axis=0):
    return tgt.at[idx].add(src)

def _segment_sum(src, seg, n):
    return jax.ops.segment_sum(src, seg, n)
kernel_name = 'mk_perceiver_d1_seqx_r4_23d271'

def setup_inputs(seed: int=0):
    np.random.seed(seed)
    _w = jnp.asarray

    def _rec_inputs():
        import jax
        import jax.numpy as jnp
        _rk = jax.random.key(seed)
        x = -0.0002928 + 1 * jax.random.normal(jax.random.fold_in(_rk, 1), (1, 128, 256), jnp.float32)
        _lenS = 128 - jax.random.randint(jax.random.fold_in(_rk, 7), (1,), 0, max(1, 128 // 4) + 1, jnp.int32)
        _lenS2 = 12544 - jax.random.randint(jax.random.fold_in(_rk, 8), (1,), 0, max(1, 12544 // 4) + 1, jnp.int32)
        _ctx_1024P = jax.random.normal(jax.random.fold_in(_rk, 11), (1, 16, 256), jnp.float32)
        _ctx_1024c = jax.random.dirichlet(jax.random.fold_in(_rk, 511), 0.3 * jnp.ones((16,), jnp.float32), (1, 12544))
        _ctx_1024t = jnp.einsum('bsk,bkd->bsd', _ctx_1024c, _ctx_1024P)
        _ctx_1024t = _ctx_1024t * jax.lax.rsqrt(jnp.mean(jnp.square(_ctx_1024t)) + 1e-12) * 0.953939
        ctx_1024 = -1.39393e-06 + 0.999914 * (_ctx_1024t + 0.3 * jax.random.normal(jax.random.fold_in(_rk, 611), (1, 12544, 256), jnp.float32))
        return (x, ctx_1024)
    x, ctx_1024 = _rec_inputs()

    def _L0_xattn_setup():
        import jax, jax.numpy as jnp
        import numpy as np
        D_MODEL, N_HEADS, RANK, TOPK = (256, 16, 32, 32)
        D_HEAD = D_MODEL // N_HEADS

        def topk_sparse(logits, k):
            top_vals = jax.lax.top_k(logits, k)[0]
            kth = top_vals[..., -1:]
            masked = jnp.where(logits >= kth, logits, -jnp.inf)
            return jax.nn.softmax(masked, axis=-1)
        key = jax.random.key(seed)
        ks = jax.random.split(key, 12)
        B, L, S = (2, 512, 512)
        sc = 0.02
        return {'q': jax.random.normal(ks[0], (B, L, D_MODEL), jnp.float32), 'k': jax.random.normal(ks[1], (B, S, D_MODEL), jnp.float32), 'v': jax.random.normal(ks[2], (B, S, D_MODEL), jnp.float32), 'Wq': jax.random.normal(ks[3], (D_MODEL, RANK * N_HEADS), jnp.float32) * sc, 'bq': jnp.zeros((RANK * N_HEADS,), jnp.float32), 'Wk': jax.random.normal(ks[4], (D_MODEL, RANK * N_HEADS), jnp.float32) * sc, 'bk': jnp.zeros((RANK * N_HEADS,), jnp.float32), 'Wv': jax.random.normal(ks[5], (D_MODEL, D_MODEL), jnp.float32) * sc, 'bv': jnp.zeros((D_MODEL,), jnp.float32), 'Wo': jax.random.normal(ks[6], (D_MODEL, D_MODEL), jnp.float32) * sc, 'bo': jnp.zeros((D_MODEL,), jnp.float32), 'pos_bias': jnp.zeros((1, N_HEADS, 1, 1), jnp.float32)}
    _L0_xattn_all = _L0_xattn_setup()
    _L0_xattn_in = {k: v for k, v in _L0_xattn_all.items() if k in ('Wq', 'bq', 'Wk', 'bk', 'Wv', 'bv', 'Wo', 'bo', 'pos_bias')}
    del _L0_xattn_all

    def _L0_attn_setup():
        import jax, jax.numpy as jnp
        import numpy as np
        D_MODEL, D_STATE, D_CONV, D_INNER = (256, 16, 4, 512)
        BATCH, SEQLEN = (4, 512)

        def _mamba_fwd(x, W_in, conv_w, W_x, W_dt, b_dt, W_Bp, D_param, W_out):
            B, L, _ = x.shape
            xz = x @ W_in
            xc, z = jnp.split(xz, 2, axis=-1)
            xt = jnp.transpose(xc, (0, 2, 1))
            xt = jax.lax.conv_general_dilated(xt, conv_w, window_strides=(1,), padding=[(D_CONV - 1, 0)], dimension_numbers=('NCH', 'OIH', 'NCH'), feature_group_count=D_INNER)
            u = jax.nn.silu(jnp.transpose(xt, (0, 2, 1)))
            xp = u @ W_x
            dt_raw, B_raw = jnp.split(xp, 2, axis=-1)
            dt = jax.nn.softplus(dt_raw @ W_dt + b_dt)
            Bp = B_raw @ W_Bp
            dt = jnp.clip(dt, 0.0001, 1.0)
            ub = u * Bp

            def step(h, inp):
                d_t, ub_t = inp
                h = h * (1.0 - d_t) + ub_t
                return (h, h)
            _, ys = jax.lax.scan(step, jnp.zeros((B, D_INNER), x.dtype), (jnp.transpose(dt, (1, 0, 2)), jnp.transpose(ub, (1, 0, 2))))
            y = jnp.transpose(ys, (1, 0, 2)) + D_param * u
            y = y * jax.nn.silu(z)
            return y @ W_out
        key = jax.random.key(seed)
        ks = jax.random.split(key, 8)
        x = jax.random.normal(ks[0], (BATCH, SEQLEN, D_MODEL), jnp.float32)
        W_in = jax.random.normal(ks[1], (D_MODEL, 2 * D_INNER), jnp.float32) / np.float32(np.sqrt(D_MODEL))
        conv_w = jax.random.normal(ks[2], (D_INNER, 1, D_CONV), jnp.float32) * np.float32(0.3)
        W_x = jax.random.normal(ks[3], (D_INNER, 2 * D_STATE), jnp.float32) / np.float32(np.sqrt(D_INNER))
        W_dt = jax.random.normal(ks[4], (D_STATE, D_INNER), jnp.float32) / np.float32(np.sqrt(D_STATE))
        b_dt = jax.random.normal(ks[5], (D_INNER,), jnp.float32) * np.float32(0.1)
        W_Bp = jax.random.normal(ks[6], (D_STATE, D_INNER), jnp.float32) / np.float32(np.sqrt(D_STATE))
        D_param = jnp.ones((D_INNER,), jnp.float32)
        W_out = jax.random.normal(ks[7], (D_INNER, D_MODEL), jnp.float32) / np.float32(np.sqrt(D_INNER))
        return {'x': x, 'W_in': W_in, 'conv_w': conv_w, 'W_x': W_x, 'W_dt': W_dt, 'b_dt': b_dt, 'W_Bp': W_Bp, 'D_param': D_param, 'W_out': W_out}
    _L0_attn_all = _L0_attn_setup()
    _L0_attn_in = {k: v for k, v in _L0_attn_all.items() if k in ('W_in', 'conv_w', 'W_x', 'W_dt', 'b_dt', 'W_Bp', 'D_param', 'W_out')}
    del _L0_attn_all

    def _L0_ffn_setup():
        import jax, jax.numpy as jnp
        import numpy as np
        import math
        D_IN = 256
        FEATURES = (1024, 1024, 256)
        BATCH, SEQ = (8, 512)

        def _conn_dense(kernel_bool, x):
            w = jnp.where(kernel_bool, jnp.float32(1.0), jnp.float32(-1.0))
            return x @ w
        key = jax.random.key(seed)
        kx, kk0, kk1, kk2 = jax.random.split(key, 4)
        x = jax.random.normal(kx, (BATCH, SEQ, D_IN), dtype=jnp.float32)
        k0 = jax.random.randint(kk0, (2 * D_IN, FEATURES[0]), 0, 2).astype(jnp.bool_)
        k1 = jax.random.randint(kk1, (FEATURES[0], FEATURES[1]), 0, 2).astype(jnp.bool_)
        k2 = jax.random.randint(kk2, (FEATURES[1], FEATURES[2]), 0, 2).astype(jnp.bool_)
        s0 = jnp.asarray(1.0 / math.sqrt(2 * D_IN), dtype=jnp.float32)
        s1 = jnp.asarray(1.0 / math.sqrt(FEATURES[0]), dtype=jnp.float32)
        s2 = jnp.asarray(1.0 / math.sqrt(FEATURES[1]), dtype=jnp.float32)
        return {'x': x, 'k0': k0, 'k1': k1, 'k2': k2, 's0': s0, 's1': s1, 's2': s2}
    _L0_ffn_all = _L0_ffn_setup()
    _L0_ffn_in = {k: v for k, v in _L0_ffn_all.items() if k in ('k0', 'k1', 'k2', 's0', 's1', 's2')}
    del _L0_ffn_all
    return {'x': x, 'ctx_1024': ctx_1024, 'L0_xattn_Wq': _L0_xattn_in['Wq'], 'L0_xattn_bq': _L0_xattn_in['bq'], 'L0_xattn_Wk': _L0_xattn_in['Wk'], 'L0_xattn_bk': _L0_xattn_in['bk'], 'L0_xattn_Wv': _L0_xattn_in['Wv'], 'L0_xattn_bv': _L0_xattn_in['bv'], 'L0_xattn_Wo': _L0_xattn_in['Wo'], 'L0_xattn_bo': _L0_xattn_in['bo'], 'L0_xattn_pos_bias': _L0_xattn_in['pos_bias'], 'L0_attn_W_in': _L0_attn_in['W_in'], 'L0_attn_conv_w': _L0_attn_in['conv_w'], 'L0_attn_W_x': _L0_attn_in['W_x'], 'L0_attn_W_dt': _L0_attn_in['W_dt'], 'L0_attn_b_dt': _L0_attn_in['b_dt'], 'L0_attn_W_Bp': _L0_attn_in['W_Bp'], 'L0_attn_D_param': _L0_attn_in['D_param'], 'L0_attn_W_out': _L0_attn_in['W_out'], 'L0_ffn_k0': _L0_ffn_in['k0'], 'L0_ffn_k1': _L0_ffn_in['k1'], 'L0_ffn_k2': _L0_ffn_in['k2'], 'L0_ffn_s0': _L0_ffn_in['s0'], 'L0_ffn_s1': _L0_ffn_in['s1'], 'L0_ffn_s2': _L0_ffn_in['s2']}

def reference(x, ctx_1024, L0_xattn_Wq, L0_xattn_bq, L0_xattn_Wk, L0_xattn_bk, L0_xattn_Wv, L0_xattn_bv, L0_xattn_Wo, L0_xattn_bo, L0_xattn_pos_bias, L0_attn_W_in, L0_attn_conv_w, L0_attn_W_x, L0_attn_W_dt, L0_attn_b_dt, L0_attn_W_Bp, L0_attn_D_param, L0_attn_W_out, L0_ffn_k0, L0_ffn_k1, L0_ffn_k2, L0_ffn_s0, L0_ffn_s1, L0_ffn_s2):
    import jax
    import jax.numpy as jnp

    def _L0_xattn_ref(q, k, v, Wq, bq, Wk, bk, Wv, bv, Wo, bo, pos_bias):
        import jax, jax.numpy as jnp
        import numpy as np
        D_MODEL, N_HEADS, RANK, TOPK = (256, 16, 32, 32)
        D_HEAD = D_MODEL // N_HEADS

        def topk_sparse(logits, k):
            top_vals = jax.lax.top_k(logits, k)[0]
            kth = top_vals[..., -1:]
            masked = jnp.where(logits >= kth, logits, -jnp.inf)
            return jax.nn.softmax(masked, axis=-1)
        B, L, _ = q.shape
        S = k.shape[1]
        Q = (q @ Wq + bq).reshape(B, L, N_HEADS, RANK).transpose(0, 2, 1, 3)
        K = (k @ Wk + bk).reshape(B, S, N_HEADS, RANK).transpose(0, 2, 1, 3)
        V = (v @ Wv + bv).reshape(B, S, N_HEADS, D_HEAD).transpose(0, 2, 1, 3)
        scores = jnp.einsum('bhlr,bhsr->bhls', Q, K) / jnp.sqrt(jnp.float32(RANK))
        scores = scores + pos_bias
        attn = topk_sparse(scores, TOPK)
        out = jnp.einsum('bhls,bhsd->bhld', attn, V)
        out = out.transpose(0, 2, 1, 3).reshape(B, L, D_MODEL)
        return out @ Wo + bo

    def _L0_attn_ref(x, W_in, conv_w, W_x, W_dt, b_dt, W_Bp, D_param, W_out):
        import jax, jax.numpy as jnp
        import numpy as np
        D_MODEL, D_STATE, D_CONV, D_INNER = (256, 16, 4, 512)
        BATCH, SEQLEN = (4, 512)

        def _mamba_fwd(x, W_in, conv_w, W_x, W_dt, b_dt, W_Bp, D_param, W_out):
            B, L, _ = x.shape
            xz = x @ W_in
            xc, z = jnp.split(xz, 2, axis=-1)
            xt = jnp.transpose(xc, (0, 2, 1))
            xt = jax.lax.conv_general_dilated(xt, conv_w, window_strides=(1,), padding=[(D_CONV - 1, 0)], dimension_numbers=('NCH', 'OIH', 'NCH'), feature_group_count=D_INNER)
            u = jax.nn.silu(jnp.transpose(xt, (0, 2, 1)))
            xp = u @ W_x
            dt_raw, B_raw = jnp.split(xp, 2, axis=-1)
            dt = jax.nn.softplus(dt_raw @ W_dt + b_dt)
            Bp = B_raw @ W_Bp
            dt = jnp.clip(dt, 0.0001, 1.0)
            ub = u * Bp

            def step(h, inp):
                d_t, ub_t = inp
                h = h * (1.0 - d_t) + ub_t
                return (h, h)
            _, ys = jax.lax.scan(step, jnp.zeros((B, D_INNER), x.dtype), (jnp.transpose(dt, (1, 0, 2)), jnp.transpose(ub, (1, 0, 2))))
            y = jnp.transpose(ys, (1, 0, 2)) + D_param * u
            y = y * jax.nn.silu(z)
            return y @ W_out
        return _mamba_fwd(x, W_in, conv_w, W_x, W_dt, b_dt, W_Bp, D_param, W_out)

    def _L0_ffn_ref(x, k0, k1, k2, s0, s1, s2):
        import jax, jax.numpy as jnp
        import numpy as np
        import math
        D_IN = 256
        FEATURES = (1024, 1024, 256)
        BATCH, SEQ = (8, 512)

        def _conn_dense(kernel_bool, x):
            w = jnp.where(kernel_bool, jnp.float32(1.0), jnp.float32(-1.0))
            return x @ w
        h = jnp.concatenate([x, -x], axis=-1)
        h = s0 * _conn_dense(k0, h)
        h = jax.nn.relu(h) * 2
        h = s1 * _conn_dense(k1, h)
        h = jax.nn.relu(h) * 2
        h = s2 * _conn_dense(k2, h)
        return h
    x = x + _L0_xattn_ref(_layernorm(x, axis=-1), ctx_1024, ctx_1024, L0_xattn_Wq, L0_xattn_bq, L0_xattn_Wk, L0_xattn_bk, L0_xattn_Wv, L0_xattn_bv, L0_xattn_Wo, L0_xattn_bo, L0_xattn_pos_bias)
    x = x + _L0_attn_ref(_layernorm(x, axis=-1), L0_attn_W_in, L0_attn_conv_w, L0_attn_W_x, L0_attn_W_dt, L0_attn_b_dt, L0_attn_W_Bp, L0_attn_D_param, L0_attn_W_out)
    x = x + _L0_ffn_ref(_layernorm(x, axis=-1), L0_ffn_k0, L0_ffn_k1, L0_ffn_k2, L0_ffn_s0, L0_ffn_s1, L0_ffn_s2)
    return x

_drawn_inputs = setup_inputs


def setup_inputs(seed=0):
    import zlib

    import numpy as np

    out = dict(_drawn_inputs(seed))
    spreads = {'L0_xattn_bq': (0.0, 0.1),
     'L0_xattn_bk': (0.0, 0.8),
     'L0_xattn_bv': (0.0, 0.1),
     'L0_xattn_bo': (0.0, 0.1),
     'L0_xattn_pos_bias': (0.0, 0.8),
     'L0_attn_D_param': (1.0, 0.2)}
    factors = {'L0_attn_W_dt': 4.923, 'L0_attn_b_dt': 8.0}
    for name, (base, spread) in spreads.items():
        noise = np.random.default_rng([zlib.crc32(name.encode()), seed]).standard_normal(out[name].shape)
        drawn = base * np.exp(spread * noise) if base else spread * noise
        out[name] = jnp.asarray(drawn.astype(out[name].dtype))
    for name, factor in factors.items():
        out[name] = (out[name] * factor).astype(out[name].dtype)
    return out
```

```python
import math
from contextlib import ExitStack

import concourse.bass as bass
from concourse import mybir

FP32 = mybir.dt.float32
BF16 = mybir.dt.bfloat16
U8 = mybir.dt.uint8
I32 = mybir.dt.int32
ACT = mybir.ActivationFunctionType
ALU = mybir.AluOpType
AX = mybir.AxisListType

P = 128
D = 256
DK = D // P
H = 16
R = 32
DH = D // H
VW = DH + 1
TOPK = 32
S_LEN = 12544
TC = 7
TW = TC * P
HW = TW // 2
NT = S_LEN // TW
SUB = HW // 2
NSUB = TW // SUB
G = H * R // P
NSPLIT = 4
KRING = 7
C0 = 4
C1 = TC - C0
DI = 512
DS = 16
CI = DI // P
TAPS = 4
F1 = 1024
NEG = -3.0e38
EPS = 1e-5
LINKS = 11


def perceiver_block(nc, a, out):
    ctx = ExitStack()
    with ctx:
        def sb(name, shape, dt=FP32):
            return ctx.enter_context(nc.sbuf_tensor(name, shape, dt))

        def pb(name, shape):
            return ctx.enter_context(nc.psum_tensor(name, shape, FP32))

        def sem(name):
            return ctx.enter_context(nc.semaphore(name))

        key_rows = nc.dram_tensor("key_rows", (H * R * NSPLIT, S_LEN), BF16, kind="Internal").ap()
        key_parts = key_rows.rearrange("(n s) c -> n s c", s=NSPLIT)
        qry_rows = nc.dram_tensor("qry_rows", (H * R * NSPLIT, 2, P), BF16, kind="Internal").ap()
        qry_parts = qry_rows.rearrange("(g p s) b q -> p g s b q", g=G, s=NSPLIT)

        values = sb("values", [P, S_LEN // P, H * VW])
        values4 = values[:, :, :].rearrange("p c (h w) -> p c h w", w=VW)
        scores = sb("scores", [P, NT * TW])
        kring = sb("kring", [P, KRING * TW], BF16)
        probs = sb("probs", [P, 2, TW])
        pt0 = sb("pt0", [P, C0 * P])
        pt1 = sb("pt1", [P, C1 * P])
        qstack = sb("qstack", [P, H, 2, P], BF16)
        cand = sb("cand", [P, NT * NSUB * 8])
        merge = sb("merge", [P, TOPK + SUB])
        top = sb("top", [P, TOPK])
        x0 = sb("x0", [P, D])
        xn = sb("xn", [P, D])
        xnT = sb("xnT", [P, DK, P])
        att = sb("att", [P, D])
        wo = sb("wo", [P, DK, D])
        bo_bc = sb("bo_bc", [P, D])
        ident = sb("ident", [P, P])
        stats = sb("stats", [P, 6])
        mv = sb("mv", [P, 2])
        rstd = sb("rstd", [P, 2])
        bq = sb("bq", [P, G])
        bk = sb("bk", [P, G])
        pos = sb("pos", [P, H])
        nbias = sb("nbias", [P, 2])
        thr = sb("thr", [P, 2])
        rowmax = sb("rowmax", [P, 2])
        flag = sb("flag", [P, 2])
        flag_i = sb("flag_i", [1, 1], I32)
        ones = sb("ones", [P, 1])
        rsum = sb("rsum", [P, 1])
        cw = sb("cw", [P, CI, TAPS])
        wx = sb("wx", [P, CI, 2 * DS])
        wdt = sb("wdt", [DS, DI])
        wbp = sb("wbp", [DS, DI])
        bdt = sb("bdt", [P, CI])
        dpar = sb("dpar", [P, CI])
        sc = sb("sc", [P, 3])

        def view(base, at, n):
            return base[:, at:at + n]

        ctx_sb = [view(scores, i * TC * D, TC * D).rearrange("p (c d) -> p c d", c=TC) for i in range(2)]
        at = 2 * TC * D
        ctxT = [view(scores, at + i * DK * TW, DK * TW).rearrange("p (k n) -> p k n", k=DK) for i in range(2)]
        at += 2 * DK * TW
        rest = [view(scores, at + i * TW, TW) for i in range(2)]
        at += 2 * TW
        half = TW // 2
        part1 = [view(scores, at + g * half, half).bitcast(BF16) for g in range(G)]
        at += G * half
        pflat = probs[:, :, :].rearrange("p a n -> p (a n)")
        wk = view(pflat, 0, DK * G * P).rearrange("p (k n) -> p k n", k=DK)
        wv = view(pflat, DK * G * P, DK * D).rearrange("p (k n) -> p k n", k=DK)
        part2 = [view(kring[:, :], g * TW, TW) for g in range(G)]
        part3 = [pt0[:, 0:half].bitcast(BF16), view(kring[:, :], 4 * TW, TW), view(kring[:, :], 5 * TW, TW),
                 view(kring[:, :], 6 * TW, TW)]
        bv_bc = view(scores, at, D)
        at += D
        wq = view(scores, at, DK * G * P).rearrange("p (k n) -> p k n", k=DK)
        at += DK * G * P
        assert at <= NT * TW, at
        vflat = values[:, :, :].rearrange("p c n -> p (c n)")
        qf = view(vflat, 0, G * P)
        qrest = view(vflat, G * P, G * P)
        qpart = [view(vflat, (2 + i) * G * P, G * P // 2).bitcast(BF16) for i in range(3)]
        qzero = view(vflat, 5 * G * P, G * P // 2).bitcast(BF16)

        kflat = kring[:, :].bitcast(FP32)
        w_in = view(kflat, 0, DK * 2 * DI).rearrange("p (k n) -> p k n", k=DK)
        w_out = view(kflat, DK * 2 * DI, CI * D).rearrange("p (k n) -> p k n", k=CI)
        vt = [0]

        def room(n):
            v = view(vflat, vt[0], n)
            vt[0] += n
            return v

        x1, x1n, x2, x2n, fin = room(D), room(D), room(D), room(D), room(D)
        x1nT = room(D).rearrange("p (k n) -> p k n", k=DK)
        x2nT = room(D).rearrange("p (k n) -> p k n", k=DK)
        attT = room(D).rearrange("p (k n) -> p k n", k=DK)
        xpad = room(CI * (P + TAPS)).rearrange("p (c n) -> p c n", c=CI)
        c4 = lambda: room(CI * P).rearrange("p (c n) -> p c n", c=CI)
        z_sb, conv, conv2, u, e1, e2, dt, sp, absd, keep, hs, y, bp, ub, sz = [c4() for _ in range(15)]
        xp = room(2 * P).rearrange("p (b n) -> p b n", b=2)
        FT = F1 // P
        f32h = [room(FT * P) for _ in range(2)]
        frest = room(FT * P)
        hp = [[room(FT * P // 2).bitcast(BF16) for _ in range(3)] for _ in range(3)]
        assert vt[0] <= (S_LEN // P) * H * VW
        K0R, K1R, K2R = 2 * D // P, F1 // P, F1 // P
        w8n = (K0R * F1 + K1R * F1 + K2R * D) // 4
        w8 = view(scores, 0, w8n).bitcast(U8)
        wbn = (K0R * F1 + K1R * F1 + K2R * D) // 2
        W8T = -(-w8n // TW)
        wb = view(scores, W8T * TW, wbn).bitcast(BF16)
        assert W8T * TW + wbn <= NT * TW
        o1, o2 = K0R * F1, (K0R + K1R) * F1
        w0b = wb[:, 0:o1].rearrange("p (k n) -> p k n", k=K0R)
        w1b = wb[:, o1:o2].rearrange("p (k n) -> p k n", k=K1R)
        w2b = wb[:, o2:o2 + K2R * D].rearrange("p (k n) -> p k n", k=K2R)

        psA = [pb(f"psA{i}", [P, 2, 512]) for i in range(2)]
        psT = pb("psT", [P, 2, 512])
        psTf = psT[:, :, :].rearrange("p a n -> p (a n)")
        psO = pb("psO", [P, 512])
        psM = pb("psM", [P, 512])

        s_ld = sem("small_loads")
        s_ctx = [sem(f"ctx_in{i}") for i in range(2)]
        s_wload = sem("weights_in")
        s_id = sem("identity_ready")
        s_one = sem("ones_ready")
        s_ln = sem("ln_chain")
        s_sq = sem("ln_sqrt")
        s_sv = sem("ln_var_ready")
        s_xn = sem("xn_ready")
        s_xt = sem("xn_transposed")
        s_xc = sem("xnT_ready")
        s_qm = sem("q_projected")
        s_qp = sem("q_parts_ready")
        s_qw = sem("q_rows_written")
        s_qs = sem("q_stack_loaded")
        s_tp = sem("ctx_transposed")
        s_ct = sem("ctxT_ready")
        s_kp = sem("key_projected")
        s_k1 = sem("key_part1_ready")
        s_r = sem("key_rest_ready")
        s_k2 = sem("key_part2_ready")
        s_k3 = sem("key_part3_ready")
        s_kw = [sem(f"key_rows_written{g}") for g in range(G)]
        s_vm = sem("values_projected")
        s_v = sem("values_ready")
        s_kin = [sem(f"key_tile_in{i}") for i in range(KRING)]
        s_mm = sem("scores_in_psum")
        s_cp = sem("scores_in_sbuf")
        s_exp = sem("exp_ready")
        s_msk = sem("masked_ready")
        s_t0 = sem("probsT_bank0")
        s_t1 = sem("probsT_bank1")
        s_e0 = sem("pt0_ready")
        s_e1 = sem("pt1_ready")
        s_pv0 = sem("pv_part0")
        s_pv1 = sem("pv_part1")
        s_max = sem("candidates_ready")
        s_lk = sem("threshold_chain")
        s_thr = sem("threshold_ready")
        s_fl = sem("flag_ready")
        s_fs = sem("flag_summed")
        s_fi = sem("flag_int_ready")
        s_gen = sem("general_path_chain")
        s_rc = sem("rowsum_inverse")
        s_oev = sem("head_output_taken")
        s_w3 = sem("state_weights_in")
        s_w8 = sem("ffn_bytes_in")
        s_wb = sem("ffn_weights_ready")
        s_dv = sem("tail_vector_chain")
        T = {n: sem(n) for n in (
            "att_turned", "attT_ready", "wo_done", "var1", "std1", "x1n_ready", "x1n_turned", "x1nT_ready",
            "xc_done", "z_done", "conv_ready", "u_exp", "z_exp", "u_ready", "low_rank_done", "xp_ready", "dt_done",
            "bp_done", "abs_ready", "dt_exp", "dt_exp1", "dt_ln", "y_ready", "mix_done", "var2", "std2", "x2n_ready",
            "x2n_turned", "x2nT_ready", "in_parts", "ffn0_done", "h0_parts", "ffn1_done", "h1_parts", "ffn2_done",
            "z_taken", "output")}
        s_out = sem("output_written")

        block = ctx.enter_context(nc.Block())
        SMALL = 15

        def flat(v):
            return v.rearrange("p c n -> p (c n)")

        def scalar_tail(act):
            def wait(n):
                act.wait_ge(T[n], 1)

            def f(dst, src, func, done, **kw):
                nc.scalar.activation(dst, src, func, **kw).then_inc(T[done], 1)

            wait("att_turned")
            f(flat(attT), psM[:, 0:D], ACT.Copy, "attT_ready")
            wait("var1")
            f(rstd[:, 0:1], mv[:, 1:2], ACT.Sqrt, "std1")
            wait("x1n_turned")
            f(flat(x1nT), psM[:, 0:D], ACT.Copy, "x1nT_ready")
            wait("z_done")
            f(flat(z_sb), psA[1][:, 0, :], ACT.Copy, "z_taken")
            wait("z_taken")
            f(flat(e2), flat(z_sb), ACT.Exp, "z_exp", scale=-1.0)
            wait("conv_ready")
            f(flat(e1), flat(conv), ACT.Exp, "u_exp", scale=-1.0)
            wait("abs_ready")
            f(flat(sp), flat(absd), ACT.Exp, "dt_exp", scale=-1.0)
            wait("dt_exp1")
            f(flat(sp), flat(sp), ACT.Ln, "dt_ln")
            wait("var2")
            f(rstd[:, 0:1], mv[:, 1:2], ACT.Sqrt, "std2")
            wait("x2n_turned")
            f(flat(x2nT), psM[:, 0:D], ACT.Copy, "x2nT_ready")

        def tensor_tail(pe):
            def turn_rows(src, ready, done):
                pe.wait_ge(*ready)
                for k in range(DK):
                    last = nc.tensor.transpose(psM[:, k * P:(k + 1) * P], src[:, k * P:(k + 1) * P], ident[:, :])
                last.then_inc(T[done], 1)

            turn_rows(att, (s_oev, H + 1), "att_turned")
            pe.wait_ge(T["attT_ready"], 1)
            for k in range(DK):
                last = nc.tensor.matmul(psO[:, 0:D], attT[:, k, :], wo[:, k, :], start=(k == 0), stop=(k == DK - 1))
            last.then_inc(T["wo_done"], 1)
            turn_rows(x1n, (T["x1n_ready"], 1), "x1n_turned")
            pe.wait_ge(T["x1nT_ready"], 1)
            pe.wait_ge(s_w3, 32)
            for j, done in enumerate(("xc_done", "z_done")):
                for c in range(CI):
                    for k in range(DK):
                        col = j * DI + c * P
                        last = nc.tensor.matmul(psA[j][:, 0, c * P:(c + 1) * P], w_in[:, k, col:col + P], x1nT[:, k, :],
                                                start=(k == 0), stop=(k == DK - 1))
                last.then_inc(T[done], 1)
            pe.wait_ge(T["u_ready"], 1)
            for j in range(2):
                for c in range(CI):
                    last = nc.tensor.matmul(psM[0:DS, j * P:(j + 1) * P], wx[:, c, j * DS:(j + 1) * DS], u[:, c, :],
                                            start=(c == 0), stop=(c == CI - 1))
            last.then_inc(T["low_rank_done"], 1)
            pe.wait_ge(T["xp_ready"], 1)
            for j, (w, done) in enumerate(((wdt, "dt_done"), (wbp, "bp_done"))):
                for c in range(CI):
                    last = nc.tensor.matmul(psT[:, j, c * P:(c + 1) * P], w[:, c * P:(c + 1) * P], xp[0:DS, j, :],
                                            start=True, stop=True)
                last.then_inc(T[done], 1)
            pe.wait_ge(T["y_ready"], 1)
            for c in range(CI):
                last = nc.tensor.matmul(psO[:, 0:D], y[:, c, :], w_out[:, c, :], start=(c == 0), stop=(c == CI - 1))
            last.then_inc(T["mix_done"], 1)
            turn_rows(x2n, (T["x2n_ready"], 1), "x2n_turned")

            def layer(w, rows, parts, ps, done):
                for ft in range(F1 // P):
                    for k in range(rows):
                        for i in range(3):
                            last = nc.tensor.matmul(ps[:, ft // 4, (ft % 4) * P:(ft % 4 + 1) * P],
                                                    w[:, k, ft * P:(ft + 1) * P], parts[i][:, k * P:(k + 1) * P],
                                                    start=(k == 0 and i == 0), stop=(k == rows - 1 and i == 2))
                last.then_inc(T[done], 1)

            pe.wait_ge(s_wb, 1)
            pe.wait_ge(T["in_parts"], 1)
            layer(w0b, K0R, hp[0], psA[0], "ffn0_done")
            pe.wait_ge(s_wb, 3)
            pe.wait_ge(T["h0_parts"], 1)
            layer(w1b, K1R, hp[1], psA[1], "ffn1_done")
            pe.wait_ge(T["h1_parts"], 1)
            for k in range(K2R):
                for i in range(3):
                    last = nc.tensor.matmul(psO[:, 0:D], hp[2][i][:, k * P:(k + 1) * P], w2b[:, k, :],
                                            start=(k == 0 and i == 0), stop=(k == K2R - 1 and i == 2))
            last.then_inc(T["ffn2_done"], 1)

        def vector_tail(dve):
            cnt = [0]

            def link(ins):
                cnt[0] += 1
                ins.then_inc(s_dv, 1)
                dve.wait_ge(s_dv, cnt[0])

            def each(make):
                for c in range(CI):
                    cnt[0] += 1
                    make(c).then_inc(s_dv, 1)
                dve.wait_ge(s_dv, cnt[0])

            V = nc.vector

            def norm(src, dst, var, std, ready):
                link(V.bn_stats(stats[:, :], src))
                link(V.bn_aggr(mv[:, :], stats[:, :]))
                V.tensor_scalar(mv[:, 1:2], mv[:, 1:2], EPS, None, ALU.add).then_inc(T[var], 1)
                dve.wait_ge(T[std], 1)
                link(V.reciprocal(rstd[:, 1:2], rstd[:, 0:1]))
                V.tensor_scalar(dst, src, mv[:, 0:1], rstd[:, 1:2], ALU.subtract, ALU.mult).then_inc(T[ready], 1)

            link(V.memset(flat(xpad), 0.0))
            dve.wait_ge(T["wo_done"], 1)
            link(V.tensor_tensor(out=x1, in0=psO[:, 0:D], in1=bo_bc[:, :], op=ALU.add))
            link(V.tensor_tensor(out=x1, in0=x1, in1=x0[:, :], op=ALU.add))
            norm(x1, x1n, "var1", "std1", "x1n_ready")
            dve.wait_ge(T["xc_done"], 1)
            link(V.tensor_copy(xpad[:, :, TAPS:], psA[0][:, 0, :].rearrange("p (c n) -> p c n", c=CI)))
            src = None
            for j in range(TAPS):
                dst = conv if j % 2 else conv2
                if j == 0:
                    each(lambda c: V.tensor_scalar(dst[:, c, :], xpad[:, c, 1:1 + P], cw[:, c, 0:1], None, ALU.mult))
                else:
                    each(lambda c: V.scalar_tensor_tensor(out=dst[:, c, :], in0=xpad[:, c, 1 + j:1 + j + P],
                                                          scalar=cw[:, c, j:j + 1], in1=src[:, c, :], op0=ALU.mult,
                                                          op1=ALU.add))
                src = dst
            V.engine_nop().then_inc(T["conv_ready"], 1)
            dve.wait_ge(T["u_exp"], 1)
            link(V.tensor_scalar(flat(e1), flat(e1), 1.0, None, ALU.add))
            link(V.reciprocal(flat(e1), flat(e1)))
            V.tensor_tensor(out=flat(u), in0=flat(conv), in1=flat(e1), op=ALU.mult).then_inc(T["u_ready"], 1)
            dve.wait_ge(T["z_exp"], 1)
            link(V.tensor_scalar(flat(e2), flat(e2), 1.0, None, ALU.add))
            link(V.reciprocal(flat(e2), flat(e2)))
            link(V.tensor_tensor(out=flat(sz), in0=flat(z_sb), in1=flat(e2), op=ALU.mult))
            dve.wait_ge(T["low_rank_done"], 1)
            V.tensor_copy(xp[0:DS, :, :], psM[0:DS, 0:2 * P].rearrange("p (b n) -> p b n", b=2))\
                .then_inc(T["xp_ready"], 1)
            dve.wait_ge(T["dt_done"], 1)
            each(lambda c: V.tensor_scalar(dt[:, c, :], psT[:, 0, c * P:(c + 1) * P], bdt[:, c:c + 1], None, ALU.add))
            link(V.tensor_scalar(flat(e1), flat(dt), -1.0, None, ALU.mult))
            V.tensor_tensor(out=flat(absd), in0=flat(dt), in1=flat(e1), op=ALU.max).then_inc(T["abs_ready"], 1)
            dve.wait_ge(T["bp_done"], 1)
            dve.wait_ge(T["u_ready"], 1)
            link(V.tensor_tensor(out=flat(ub), in0=psT[:, 1, :], in1=flat(u), op=ALU.mult))
            dve.wait_ge(T["dt_exp"], 1)
            V.tensor_scalar(flat(sp), flat(sp), 1.0, None, ALU.add).then_inc(T["dt_exp1"], 1)
            dve.wait_ge(T["dt_ln"], 1)
            link(V.scalar_tensor_tensor(out=flat(dt), in0=flat(dt), scalar=0.0, in1=flat(sp), op0=ALU.max,
                                        op1=ALU.add))
            link(V.tensor_scalar(flat(dt), flat(dt), 1e-4, 1.0, ALU.max, ALU.min))
            link(V.tensor_scalar(flat(keep), flat(dt), -1.0, 1.0, ALU.mult, ALU.add))
            each(lambda c: V.tensor_tensor_scan(hs[:, c, :], keep[:, c, :], ub[:, c, :], 0.0, ALU.mult, ALU.add))
            each(lambda c: V.scalar_tensor_tensor(out=y[:, c, :], in0=u[:, c, :], scalar=dpar[:, c:c + 1],
                                                  in1=hs[:, c, :], op0=ALU.mult, op1=ALU.add))
            V.tensor_tensor(out=flat(y), in0=flat(y), in1=flat(sz), op=ALU.mult).then_inc(T["y_ready"], 1)
            dve.wait_ge(T["mix_done"], 1)
            link(V.tensor_tensor(out=x2, in0=psO[:, 0:D], in1=x1, op=ALU.add))
            norm(x2, x2n, "var2", "std2", "x2n_ready")

            def parts(src, n, dst, r):
                link(V.tensor_copy(dst[0][:, 0:n], src))
                link(V.tensor_tensor(out=r, in0=src, in1=dst[0][:, 0:n], op=ALU.subtract))
                link(V.tensor_copy(dst[1][:, 0:n], r))
                link(V.tensor_tensor(out=dst[2][:, 0:n], in0=r, in1=dst[1][:, 0:n], op=ALU.subtract))

            dve.wait_ge(T["x2nT_ready"], 1)
            parts(flat(x2nT), D, hp[0], frest[:, 0:D])
            for i in range(3):
                link(V.tensor_scalar(hp[0][i][:, D:2 * D], hp[0][i][:, 0:D], -1.0, None, ALU.mult))
            V.engine_nop().then_inc(T["in_parts"], 1)
            for i, (ps, ready, done) in enumerate(((psA[0], "ffn0_done", "h0_parts"), (psA[1], "ffn1_done", "h1_parts"))):
                dve.wait_ge(T[ready], 1)
                psf = ps[:, :, :].rearrange("p a n -> p (a n)")
                link(V.tensor_scalar(f32h[i], psf, sc[:, i:i + 1], 0.0, ALU.mult, ALU.max))
                link(V.tensor_scalar(f32h[i], f32h[i], 2.0, None, ALU.mult))
                parts(f32h[i], F1, hp[i + 1], frest)
                V.engine_nop().then_inc(T[done], 1)
            dve.wait_ge(T["ffn2_done"], 1)
            V.scalar_tensor_tensor(out=fin, in0=psO[:, 0:D], scalar=sc[:, 2:3], in1=x2, op0=ALU.mult,
                                   op1=ALU.add).then_inc(T["output"], 1)

        @block.sync
        def _(sp):
            sp.dma_start(x0[:, :], a["x"][0]).then_inc(s_ld, 16)
            def load_ctx(t, i):
                src = a["ctx_1024"][0][bass.ds(t * TW, TW), :] if not isinstance(t, int) \
                    else a["ctx_1024"][0][t * TW:(t + 1) * TW, :]
                sp.dma_start(ctx_sb[i], src.rearrange("(c p) d -> p c d", p=P)).then_inc(s_ctx[i], 16)

            sp.dma_start(wq, a["L0_xattn_Wq"].rearrange("(k p) n -> p k n", p=P)).then_inc(s_wload, 16)
            load_ctx(0, 0)
            sp.dma_start(wk, a["L0_xattn_Wk"].rearrange("(k p) n -> p k n", p=P)).then_inc(s_wload, 16)
            load_ctx(1, 1)
            sp.dma_start(wv, a["L0_xattn_Wv"].rearrange("(k p) n -> p k n", p=P)).then_inc(s_wload, 16)
            sp.wait_ge(s_qp, 2)
            places = {(0, 0): 0, (1, 0): 0, (2, 0): 0, (3, 0): 1, (0, 1): 2, (1, 1): 1, (2, 1): 1, (3, 1): 3}
            for (s, b), i in places.items():
                src = (qpart + [qzero])[i].rearrange("p (g q) -> p g q", g=G)
                sp.dma_start(qry_parts[:, :, s, b, :], src).then_inc(s_qw, 16)
            sp.wait_ge(s_qw, 16 * len(places))
            sp.dma_start(qstack[:, :, :, :], qry_rows.rearrange("(h p) b q -> p h b q", p=P)).then_inc(s_qs, 16)

            def key_writes(t, last=False):
                for g in range(G):
                    u = G * t + g
                    cols = bass.ds(t * TW, TW)
                    rows = slice(g * P, (g + 1) * P)
                    sp.wait_ge(s_k1, u + 1)
                    sp.dma_start(key_parts[rows, 0, cols], part1[g]).then_inc(s_kw[g], 16)
                    sp.dma_start(key_parts[rows, 3, cols], part1[g]).then_inc(s_kw[g], 16)
                    sp.wait_ge(s_k2, u + 1)
                    sp.dma_start(key_parts[rows, 1, cols], part2[g]).then_inc(s_kw[g], 16)
                    sp.wait_ge(s_k3, u + 1)
                    sp.dma_start(key_parts[rows, 2, cols], part3[g]).then_inc(s_kw[g], 16)

            with sp.Fori(0, NT // 2 - 1) as i:
                for j in range(2):
                    key_writes(2 * i + j)
                    sp.wait_ge(s_tp, 2 * (2 * i + j + 1))
                    load_ctx(2 * i + j + 2, j)
            for t in range(NT - 2, NT):
                key_writes(t)
            for g in range(G):
                sp.wait_ge(s_kw[g], 4 * 16 * NT)

            def stream(h, t):
                sp.dma_start(kring[:, (t % KRING) * TW:(t % KRING + 1) * TW],
                             key_rows[bass.ds(h * P, P), t * TW:(t + 1) * TW]).then_inc(s_kin[t % KRING], 16)

            for t in range(KRING):
                stream(0, t)
            for t in range(KRING, NT):
                sp.wait_ge(s_mm, t - KRING + 1)
                stream(0, t)
            with sp.Fori(1, H) as h:
                for t in range(NT):
                    sp.wait_ge(s_mm, h * NT + (t - KRING + 1))
                    stream(h, t)
            sp.wait_ge(s_mm, H * NT)
            sp.dma_start(w_in, a["L0_attn_W_in"].rearrange("(k p) n -> p k n", p=P)).then_inc(s_w3, 16)
            sp.dma_start(w_out, a["L0_attn_W_out"].rearrange("(k p) n -> p k n", p=P)).then_inc(s_w3, 16)
            sp.wait_ge(s_msk, (H - 1) * NT + W8T)
            for k, lo, rows, n in (("L0_ffn_k0", 0, K0R, F1), ("L0_ffn_k1", o1, K1R, F1), ("L0_ffn_k2", o2, K2R, D)):
                sp.dma_start(w8[:, lo:lo + rows * n].rearrange("p (k n) -> p k n", k=rows),
                             a[k].rearrange("(k p) n -> p k n", p=P)).then_inc(s_w8, 16)
            sp.wait_ge(T["output"], 1)
            sp.dma_start(out[0], fin).then_inc(s_out, 16)
            sp.wait_ge(s_out, 16)

        @block.gpsimd
        def _(pool):
            nc.gpsimd.memset(ident[:, :], 0.0).then_inc(s_id, 1)
            nc.gpsimd.memset(ones[:, :], 1.0).then_inc(s_one, 1)
            pool.wait_ge(s_id, 1)
            nc.gpsimd.affine_select(out=ident[:, :], in_=ident[:, :], compare_op=ALU.not_equal, fill=1.0, base=0,
                                    pattern=[[-1, P]], channel_multiplier=1).then_inc(s_id, 1)
            pool.wait_ge(s_qw, 16 * 8)
            nc.gpsimd.memset(values4[:, :, :, DH:VW], 1.0).then_inc(s_one, 1)

            def split(t, g):
                u = G * t + g
                pool.wait_ge(s_r, u + 3)
                if not isinstance(t, int):
                    pool.wait_ge(s_kw[g], 64 * t)
                    pool.nop(nofuse=True)
                nc.gpsimd.tensor_copy(part2[g], rest[g % 2]).then_inc(s_k2, 1)
                pool.wait_ge(s_k2, u + 1)
                nc.gpsimd.tensor_tensor(out=part3[g], in0=rest[g % 2], in1=part2[g],
                                        op=ALU.subtract).then_inc(s_k3, 1)

            for g in range(G):
                split(0, g)
            with pool.Fori(1, NT) as t:
                for g in range(G):
                    split(t, g)
            pool.wait_ge(s_w8, 48)
            pool.wait_ge(s_msk, H * NT)
            for lo, n in ((0, o1), (o1, o2 - o1), (o2, K2R * D)):
                nc.gpsimd.tensor_scalar(wb[:, lo:lo + n], w8[:, lo:lo + n], 2.0, -1.0, ALU.mult,
                                        ALU.add).then_inc(s_wb, 1)

        @block.scalar
        def _(act):
            def bcast(dst, src, n):
                act.dma_start(dst, src.rearrange("(o n) -> o n", o=1).broadcast_to([P, n])).then_inc(s_ld, 16)

            def cols(dst, src):
                act.dma_start(dst, src.rearrange("(g p) -> p g", p=P), allow_slow_non_contiguous=True).then_inc(s_ld, 16)

            cols(bq[:, :], a["L0_xattn_bq"])
            cols(bk[:, :], a["L0_xattn_bk"])
            bcast(bv_bc, a["L0_xattn_bv"], D)
            bcast(bo_bc[:, :], a["L0_xattn_bo"], D)
            bcast(pos[:, :], a["L0_xattn_pos_bias"].rearrange("a h b c -> (a h b c)"), H)
            act.dma_start(wo[:, :, :], a["L0_xattn_Wo"].rearrange("(k p) n -> p k n", p=P)).then_inc(s_ld, 16)
            act.dma_start(cw[:, :, :], a["L0_attn_conv_w"].rearrange("(c p) o k -> p c (o k)", p=P)).then_inc(s_ld, 16)
            act.dma_start(wx[:, :, :], a["L0_attn_W_x"].rearrange("(c p) n -> p c n", p=P)).then_inc(s_ld, 16)
            act.dma_start(wdt[:, :], a["L0_attn_W_dt"]).then_inc(s_ld, 16)
            act.dma_start(wbp[:, :], a["L0_attn_W_Bp"]).then_inc(s_ld, 16)
            cols(bdt[:, :], a["L0_attn_b_dt"])
            cols(dpar[:, :], a["L0_attn_D_param"])
            for i in range(3):
                act.dma_start(sc[:, i:i + 1], a[f"L0_ffn_s{i}"].rearrange("(o n) -> o n", o=1)
                              .broadcast_to([P, 1])).then_inc(s_ld, 16)
            act.wait_ge(s_sv, 1)
            nc.scalar.activation(rstd[:, 0:1], mv[:, 1:2], ACT.Sqrt).then_inc(s_sq, 1)
            act.wait_ge(s_xt, 1)
            nc.scalar.activation(xnT[:, :, :], psM[:, 0:D].rearrange("p (k n) -> p k n", k=DK),
                                 ACT.Copy).then_inc(s_xc, 1)
            act.wait_ge(s_ld, 16 * (SMALL + 1))

            def take_ctxT(t, i, k):
                act.wait_ge(s_tp, 2 * t + k + 1)
                if k == 0:
                    act.wait_ge(s_vm, TC * t)
                nc.scalar.activation(ctxT[i][:, k, :], psTf[:, 0:TW], ACT.Copy).then_inc(s_ct, 1)

            def take_part1(t, g):
                u = G * t + g
                act.wait_ge(s_kp, u + 1)
                if not (isinstance(t, int) and t == 0):
                    act.wait_ge(s_kw[g], 64 * t)
                nc.scalar.activation(part1[g].rearrange("p (a n) -> p a n", a=2), psA[g % 2][:, :, 0:HW],
                                     ACT.Identity, bias=bk[:, g:g + 1]).then_inc(s_k1, 1)

            def key_tile(t, i, more):
                if more:
                    take_ctxT(t + 1, 1 - i, 0)
                take_part1(t, 0)
                if more:
                    take_ctxT(t + 1, 1 - i, 1)
                for g in range(1, G):
                    take_part1(t, g)

            take_ctxT(0, 0, 0)
            take_ctxT(0, 0, 1)
            for t in range(2):
                key_tile(t, t, True)
            with act.Fori(1, NT // 2 - 1) as i:
                for j in range(2):
                    key_tile(2 * i + j, j, True)
            key_tile(NT - 2, 0, True)
            key_tile(NT - 1, 1, False)

            def copy_scores(hA, t):
                n = hA * NT + t
                act.wait_ge(s_mm, n + 1)
                if not (isinstance(hA, int) and hA == 0):
                    act.wait_ge(s_msk, n - NT + 1)
                elif t == 0:
                    act.wait_ge(s_vm, TC * (NT + 1))
                    act.wait_ge(s_v, TC * NT)
                    for g in range(G):
                        act.wait_ge(s_kw[g], 64 * NT)
                nc.scalar.activation(scores[:, t * TW:(t + 1) * TW].rearrange("p (a n) -> p a n", a=2),
                                     psA[t % 2][:, :, 0:HW], ACT.Copy).then_inc(s_cp, 1)

            def exps(hB, t):
                m = hB * NT + t
                if t == 0:
                    act.wait_ge(s_thr, hB + 1)
                act.wait_ge(s_t1, m + 1)
                nc.scalar.activation(probs[:, t % 2, :], scores[:, t * TW:(t + 1) * TW], ACT.Exp,
                                     bias=nbias[:, 0:1]).then_inc(s_exp, 1)

            def take_pt0(hB, t):
                m = hB * NT + t
                act.wait_ge(s_t0, m + 1)
                act.wait_ge(s_pv0, m + 1)
                nc.scalar.activation(pt0[:, :], psT[:, 0, 0:C0 * P], ACT.Copy).then_inc(s_e0, 1)

            def head(hB, hA):
                if hB is not None:
                    exps(hB, 0)
                for t in range(NT):
                    if hB is not None and t + 1 < NT:
                        exps(hB, t + 1)
                    if hA is not None:
                        copy_scores(hA, t)
                    if hB is not None:
                        take_pt0(hB, t)

            head(None, 0)
            with act.Fori(0, H - 1) as h:
                head(h, h + 1)
            head(H - 1, None)
            scalar_tail(act)

        @block.tensor
        def _(pe):
            pe.sem_inc(s_vm, TC)
            pe.sem_inc(s_t1, 2)
            pe.sem_inc(s_pv0, 1)
            pe.sem_inc(s_pv1, 1)
            pe.sem_inc(s_e0, 1)
            pe.sem_inc(s_e1, 1)
            pe.sem_inc(s_oev, 1)
            pe.wait_ge(s_id, 2)
            pe.wait_ge(s_xn, 1)
            for k in range(DK):
                last = nc.tensor.transpose(psM[:, k * P:(k + 1) * P], xn[:, k * P:(k + 1) * P], ident[:, :])
            last.then_inc(s_xt, 1)
            pe.wait_ge(s_xc, 1)
            pe.wait_ge(s_wload, 48)
            for g in range(G):
                for k in range(DK):
                    last = nc.tensor.matmul(psO[:, g * P:(g + 1) * P], wq[:, k, g * P:(g + 1) * P], xnT[:, k, :],
                                            start=(k == 0), stop=(k == DK - 1))
            last.then_inc(s_qm, 1)

            def turn_ctx(t, i, k):
                if k == 0:
                    n = (t // 2 + 1) if isinstance(t, int) else None
                    pe.wait_ge(s_ctx[i], 16 * n if n is not None else 8 * (t - i) + 16)
                pe.wait_ge(s_ct, 2 * t + k)
                for c in range(TC):
                    last = nc.tensor.transpose(psTf[:, c * P:(c + 1) * P], ctx_sb[i][:, c, k * P:(k + 1) * P],
                                               ident[:, :])
                last.then_inc(s_tp, 1)

            def project_keys(t, i, g):
                if g == 0:
                    pe.wait_ge(s_ct, 2 * t + 2)
                pe.wait_ge(s_r, G * t + g + 1)
                for a_ in range(2):
                    for k in range(DK):
                        last = nc.tensor.matmul(psA[g % 2][:, a_, 0:HW], wk[:, k, g * P:(g + 1) * P],
                                                ctxT[i][:, k, a_ * HW:(a_ + 1) * HW],
                                                start=(k == 0), stop=(k == DK - 1))
                last.then_inc(s_kp, 1)

            def project_values(t, i):
                for c in range(TC):
                    w = TC * t + c
                    bank = (psO, psM)[c % 2]
                    if c == 0 and not (isinstance(w, int) and w == 0):
                        pe.wait_ge(s_v, w)
                    elif c > 1:
                        pe.wait_ge(s_v, w - 1)
                    for k in range(DK):
                        last = nc.tensor.matmul(bank[:, 0:D], ctxT[i][:, k, c * P:(c + 1) * P], wv[:, k, :],
                                                start=(k == 0), stop=(k == DK - 1))
                    last.then_inc(s_vm, 1)

            def key_tile(t, i, more):
                if more:
                    turn_ctx(t + 1, 1 - i, 0)
                project_keys(t, i, 0)
                if more:
                    turn_ctx(t + 1, 1 - i, 1)
                for g in range(1, G):
                    project_keys(t, i, g)
                project_values(t, i)

            pe.wait_ge(s_qp, 2)
            turn_ctx(0, 0, 0)
            turn_ctx(0, 0, 1)
            for t in range(2):
                key_tile(t, t, True)
            with pe.Fori(1, NT // 2 - 1) as i:
                for j in range(2):
                    key_tile(2 * i + j, j, True)
            key_tile(NT - 2, 0, True)
            key_tile(NT - 1, 1, False)

            def score_tile(hA, t):
                n = hA * NT + t
                pe.wait_ge(s_kin[t % KRING], 16 * (2 * hA + t // KRING + 1))
                if not (isinstance(hA, int) and n < 2):
                    pe.wait_ge(s_cp, n - 1)
                for a_ in range(2):
                    cols = kring[:, (t % KRING) * TW + a_ * HW:(t % KRING) * TW + (a_ + 1) * HW]
                    for b in range(2):
                        lhsT = qstack[:, hA, b, :] if isinstance(hA, int) else qstack[:, bass.ds(hA, 1), b, :]\
                            .rearrange("p o q -> p (o q)")
                        last = nc.tensor.matmul(psA[t % 2][:, a_, 0:HW], lhsT, cols, start=(b == 0), stop=(b == 1))
                last.then_inc(s_mm, 1)

            def turn(hB, t, part):
                m = hB * NT + t
                lo, n, s_e, s_t = ((0, C0, s_e0, s_t0), (C0, C1, s_e1, s_t1))[part]
                if part == 0:
                    pe.wait_ge(s_msk, m + 1)
                pe.wait_ge(s_e, m + 1)
                for c in range(n):
                    last = nc.tensor.transpose(psT[:, part, c * P:(c + 1) * P],
                                               probs[:, t % 2, (lo + c) * P:(lo + c + 1) * P], ident[:, :])
                last.then_inc(s_t, 1)

            def weigh(hB, t, part):
                m = hB * NT + t
                lo, n, s_e, s_pv, pt = ((0, C0, s_e0, s_pv0, pt0), (C0, C1, s_e1, s_pv1, pt1))[part]
                pe.wait_ge(s_e, m + 2)
                if part == 0 and t == 0:
                    pe.wait_ge(s_oev, hB + 1)
                for c in range(n):
                    v = values[:, t * TC + lo + c, :]
                    v = v[:, hB * VW:(hB + 1) * VW] if isinstance(hB, int) else v[:, bass.ds(hB * VW, VW)]
                    last = nc.tensor.matmul(psO[:, 0:VW], pt[:, c * P:(c + 1) * P], v,
                                            start=(t == 0 and part == 0 and c == 0),
                                            stop=(t == NT - 1 and part == 1 and c == n - 1))
                last.then_inc(s_pv, 1)

            def head(hB, hA):
                if hA is not None:
                    score_tile(hA, 0)
                for t in range(NT):
                    if hB is not None:
                        turn(hB, t, 0)
                    if hA is not None and t + 1 < NT:
                        score_tile(hA, t + 1)
                    if hB is not None:
                        if t > 0:
                            weigh(hB, t - 1, 1)
                        turn(hB, t, 1)
                        weigh(hB, t, 0)
                if hB is not None:
                    weigh(hB, NT - 1, 1)
                if hA is not None:
                    pe.wait_ge(s_fl, hA + 1)
                    nc.tensor.matmul(psM[0:1, 0:1], flag[:, 0:1], ones[:, :], start=True, stop=True)\
                        .then_inc(s_fs, 1)

            pe.wait_ge(s_v, TC * NT)
            pe.wait_ge(s_one, 2)
            pe.wait_ge(s_qs, 16)
            head(None, 0)
            with pe.Fori(0, H - 1) as h:
                head(h, h + 1)
            head(H - 1, None)
            tensor_tail(pe)

        @block.vector
        def _(dve):
            dve.sem_inc(s_r, 2)
            n_ln = [0]

            def link(ins):
                n_ln[0] += 1
                ins.then_inc(s_ln, 1)
                dve.wait_ge(s_ln, n_ln[0])

            dve.wait_ge(s_ld, 16 * (SMALL + 1))
            link(nc.vector.bn_stats(stats[:, :], x0[:, :]))
            link(nc.vector.bn_aggr(mv[:, :], stats[:, :]))
            nc.vector.tensor_scalar(mv[:, 1:2], mv[:, 1:2], EPS, None, ALU.add).then_inc(s_sv, 1)
            dve.wait_ge(s_sq, 1)
            link(nc.vector.reciprocal(rstd[:, 1:2], rstd[:, 0:1]))
            nc.vector.tensor_scalar(xn[:, :], x0[:, :], mv[:, 0:1], rstd[:, 1:2], ALU.subtract,
                                    ALU.mult).then_inc(s_xn, 1)
            dve.wait_ge(s_qm, 1)
            for g in range(G):
                q = nc.vector.tensor_scalar(qf[:, g * P:(g + 1) * P], psO[:, g * P:(g + 1) * P], bq[:, g:g + 1],
                                            1.0 / math.sqrt(R), ALU.add, ALU.mult)
                link(q)
            link(nc.vector.tensor_copy(qpart[0], qf))
            link(nc.vector.tensor_tensor(out=qrest, in0=qf, in1=qpart[0], op=ALU.subtract))
            link(nc.vector.tensor_copy(qpart[1], qrest))
            nc.vector.tensor_tensor(out=qpart[2], in0=qrest, in1=qpart[1], op=ALU.subtract).then_inc(s_qp, 1)
            nc.vector.memset(qzero, 0.0).then_inc(s_qp, 1)
            dve.wait_ge(s_qw, 16 * 8)

            def key_tile(t):
                for g in range(G):
                    u = G * t + g
                    dve.wait_ge(s_k1, u + 1)
                    if not (isinstance(t, int) and u < 2):
                        dve.wait_ge(s_k3, u - 1)
                    nc.vector.scalar_tensor_tensor(
                        out=rest[g % 2].rearrange("p (a n) -> p a n", a=2), in0=psA[g % 2][:, :, 0:HW],
                        scalar=bk[:, g:g + 1], in1=part1[g].rearrange("p (a n) -> p a n", a=2),
                        op0=ALU.add, op1=ALU.subtract).then_inc(s_r, 1)
                for c in range(TC):
                    w = TC * t + c
                    dve.wait_ge(s_vm, w + 1 + TC)
                    dst = values4[:, w, :, 0:DH] if isinstance(t, int) else \
                        values4[:, bass.ds(w, 1), :, 0:DH].rearrange("p o h d -> p (o h) d")
                    nc.vector.tensor_tensor(out=dst, in0=(psO, psM)[c % 2][:, 0:D].rearrange("p (h d) -> p h d", h=H),
                                            in1=bv_bc.rearrange("p (h d) -> p h d", h=H), op=ALU.add)\
                        .then_inc(s_v, 1)

            key_tile(0)
            with dve.Fori(1, NT) as t:
                key_tile(t)

            def mask(hB, t):
                m = hB * NT + t
                dve.wait_ge(s_exp, m + 1)
                nc.vector.scalar_tensor_tensor(out=probs[:, t % 2, :], in0=scores[:, t * TW:(t + 1) * TW],
                                               scalar=thr[:, 0:1], in1=probs[:, t % 2, :], op0=ALU.is_ge,
                                               op1=ALU.mult).then_inc(s_msk, 1)

            def take_candidates(hA, t):
                n = hA * NT + t
                dve.wait_ge(s_cp, n + 1)
                dve.nop(nofuse=True)
                for j in range(NSUB):
                    i = t * NSUB + j
                    last = nc.vector.max(cand[:, 8 * i:8 * i + 8], scores[:, t * TW + j * SUB:t * TW + (j + 1) * SUB])
                last.then_inc(s_max, 1)

            def take_pt1(hB, t):
                m = hB * NT + t
                dve.wait_ge(s_t1, m + 3)
                dve.wait_ge(s_pv1, m + 1)
                nc.vector.tensor_copy(pt1[:, :], psT[:, 1, 0:C1 * P]).then_inc(s_e1, 1)

            def threshold(hA):
                step = [0]

                def chain(ins):
                    step[0] += 1
                    ins.then_inc(s_lk, 1)
                    dve.wait_ge(s_lk, hA * LINKS + step[0])
                    dve.nop(nofuse=True)

                def both(*ins):
                    for i in ins[:-1]:
                        i.then_inc(s_lk, 1)
                        step[0] += 1
                    chain(ins[-1])

                dve.wait_ge(s_max, (hA + 1) * NT)
                chain(nc.vector.tensor_reduce(flag[:, 1:2], cand[:, :].rearrange("p (s e) -> p s e", e=8)[:, :, 7:8]
                                              .rearrange("p s e -> p (s e)"), AX.X, ALU.max))
                for r in range(TOPK // 8):
                    chain(nc.vector.max(top[:, 8 * r:8 * r + 8], cand[:, :]))
                    if r + 1 < TOPK // 8:
                        chain(nc.vector.match_replace(cand[:, :], top[:, 8 * r:8 * r + 8], cand[:, :], NEG))
                nc.vector.tensor_tensor(out=flag[:, 0:1], in0=flag[:, 1:2], in1=top[:, TOPK - 1:TOPK],
                                        op=ALU.is_ge).then_inc(s_fl, 1)
                dve.wait_ge(s_fs, hA + 1)
                nc.vector.tensor_copy(flag_i[:, :], psM[0:1, 0:1]).then_inc(s_fi, 1)
                dve.wait_ge(s_fi, hA + 1)
                dve.nop(nofuse=True)
                flagged = dve.value_load(flag_i[0:1, 0:1], min_val=0, max_val=P)
                with dve.If(flagged > 0):
                    general_threshold()
                pcol = pos[:, hA:hA + 1] if isinstance(hA, int) else pos[:, bass.ds(hA, 1)]
                nc.vector.tensor_copy(thr[:, 0:1], top[:, TOPK - 1:TOPK]).then_inc(s_lk, 1)
                step[0] += 1
                chain(nc.vector.tensor_tensor(out=rowmax[:, 0:1], in0=top[:, 0:1], in1=pcol, op=ALU.add))
                assert step[0] == LINKS - 1, step[0]
                chain(nc.vector.tensor_tensor(out=nbias[:, 0:1], in0=pcol, in1=rowmax[:, 0:1], op=ALU.subtract))
                dve.sem_inc(s_thr, 1)

            def general_threshold():
                cnt = [0]

                def chain(ins):
                    cnt[0] += 1
                    ins.then_inc(s_gen, 1)
                    dve.wait_ge(s_gen, cnt[0])

                def fold(src):
                    chain(nc.vector.tensor_copy(merge[:, TOPK:TOPK + SUB], src))
                    for r in range(TOPK // 8):
                        chain(nc.vector.max(top[:, 8 * r:8 * r + 8], merge[:, :]))
                        chain(nc.vector.match_replace(merge[:, :], top[:, 8 * r:8 * r + 8], merge[:, :], NEG))
                    chain(nc.vector.tensor_copy(merge[:, 0:TOPK], top[:, :]))
                    dve.sem_clear(s_gen)
                    cnt[0] = 0

                chain(nc.vector.memset(merge[:, 0:TOPK], NEG))
                dve.sem_clear(s_gen)
                cnt[0] = 0
                with dve.Fori(0, NT * NSUB) as i:
                    fold(scores[:, bass.ds(i * SUB, SUB)])

            def take_output(hB):
                dve.wait_ge(s_pv1, (hB + 1) * NT + 1)
                nc.vector.reciprocal(rsum[:, :], psO[:, DH:VW]).then_inc(s_rc, 1)
                dve.wait_ge(s_rc, hB + 1)
                dst = att[:, hB * DH:(hB + 1) * DH] if isinstance(hB, int) else att[:, bass.ds(hB * DH, DH)]
                nc.vector.tensor_scalar(dst, psO[:, 0:DH], rsum[:, :], None, ALU.mult).then_inc(s_oev, 1)

            def head(hB, hA):
                for t in range(NT):
                    if hB is not None:
                        mask(hB, t)
                    if hA is not None and t > 0:
                        take_candidates(hA, t - 1)
                    if hB is not None:
                        take_pt1(hB, t)
                if hA is not None:
                    take_candidates(hA, NT - 1)
                if hB is not None:
                    take_output(hB)
                if hA is not None:
                    threshold(hA)

            head(None, 0)
            with dve.Fori(0, H - 1) as h:
                head(h, h + 1)
            head(H - 1, None)
            vector_tail(dve)


def kernel(**inputs):
    import numpy as _np
    import concourse.bacc as _bacc
    from concourse import mybir as _mybir
    from concourse.bass_utils import run_bass_kernel_spmd as _run

    nc = _bacc.Bacc("TRN2", target_bir_lowering=False, num_devices=1)
    arrays, handles = {}, {}
    for name, value in inputs.items():
        v = _np.ascontiguousarray(value)
        if v.ndim == 0:
            v = v.reshape(1)
        arrays[f"in_{name}"] = v
        handles[name] = nc.dram_tensor(f"in_{name}", v.shape, _mybir.dt.from_np(v.dtype), kind="ExternalInput").ap()
    out = nc.dram_tensor("out_0", (1, P, D), _mybir.dt.float32, kind="ExternalOutput").ap()
    perceiver_block(nc, handles, out)
    r = _run(nc, [arrays], core_ids=[0])
    return r.results[0]["out_0"]
```

```python
import math
from contextlib import ExitStack

import concourse.bass as bass
from concourse import mybir

FP32 = mybir.dt.float32
BF16 = mybir.dt.bfloat16
U8 = mybir.dt.uint8
I32 = mybir.dt.int32
ACT = mybir.ActivationFunctionType
ALU = mybir.AluOpType
AX = mybir.AxisListType

P = 128
D = 256
DK = D // P
H = 16
R = 32
DH = D // H
VW = DH + 1
TOPK = 32
S_LEN = 12544
TC = 7
TW = TC * P
HW = TW // 2
NT = S_LEN // TW
SUB = HW // 2
NSUB = TW // SUB
G = H * R // P
NSPLIT = 4
KRING = 7
C0 = 4
QUAD = 32
NQ = P // QUAD
DI = 512
DS = 16
CI = DI // P
TAPS = 4
F1 = 1024
NEG = -3.0e38
EPS = 1e-5
LINKS = 11
FLAG_T = 10


def perceiver_block(nc, a, out):
    ctx = ExitStack()
    with ctx:
        def sb(name, shape, dt=FP32):
            return ctx.enter_context(nc.sbuf_tensor(name, shape, dt))

        def pb(name, shape):
            return ctx.enter_context(nc.psum_tensor(name, shape, FP32))

        def sem(name):
            return ctx.enter_context(nc.semaphore(name))

        key_rows = nc.dram_tensor("key_rows", (H * R * NSPLIT, S_LEN), BF16, kind="Internal").ap()
        key_parts = key_rows.rearrange("(n s) c -> n s c", s=NSPLIT)
        qry_rows = nc.dram_tensor("qry_rows", (H * R * NSPLIT, 2, P), BF16, kind="Internal").ap()
        value_rows = nc.dram_tensor("value_rows", (H, P, S_LEN // P * VW), FP32, kind="Internal").ap()
        qry_parts = qry_rows.rearrange("(g p s) b q -> p g s b q", g=G, s=NSPLIT)

        scores2 = sb("scores", [P, 2, NT * TW])
        vhead = sb("vhead", [P, 2, S_LEN // P, VW])
        outT = sb("outT", [P, H + 1, P])
        select = sb("select", [P, VW])
        kring = sb("kring", [P, KRING * TW], BF16)
        probs = sb("probs", [P, 2, TW])
        pt = sb("pt", [P, 2, TW])
        qstack = sb("qstack", [P, H, 2, P], BF16)
        cand = sb("cand", [P, 2, NT * NSUB * 8])
        merge = sb("merge", [P, TOPK + SUB])
        top = sb("top", [P, TOPK])
        x0 = sb("x0", [P, D])
        xn = sb("xn", [P, D])
        xnT = sb("xnT", [P, DK, P])
        att = sb("att", [P, D])
        wo = sb("wo", [P, DK, D])
        bo_bc = sb("bo_bc", [P, D])
        ident = sb("ident", [P, P])
        stats = sb("stats", [P, 6])
        mv = sb("mv", [P, 2])
        rstd = sb("rstd", [P, 2])
        bq = sb("bq", [P, G])
        bk = sb("bk", [P, G])
        pos = sb("pos", [P, H])
        nbias = sb("nbias", [P, 2])
        thr = sb("thr", [P, 2])
        rowmax = sb("rowmax", [P, 2])
        flag = sb("flag", [P, 2])
        flag_i = sb("flag_i", [1, 1], I32)
        ones = sb("ones", [P, 1])
        rsum = sb("rsum", [P, H])
        cw = sb("cw", [P, CI, TAPS])
        wx = sb("wx", [P, CI, 2 * DS])
        wdt = sb("wdt", [DS, DI])
        wbp = sb("wbp", [DS, DI])
        bdt = sb("bdt", [P, CI])
        dpar = sb("dpar", [P, CI])
        sc = sb("sc", [P, 3])

        sflat = scores2[:, :, :].rearrange("p a n -> p (a n)")
        at = [0]

        def view(base, lo, n):
            return base[:, lo:lo + n]

        def place(n):
            v = view(sflat, at[0], n)
            at[0] += n
            return v

        half = TW // 2
        ctx_sb = [place(TC * D).rearrange("p (c d) -> p c d", c=TC) for _ in range(2)]
        ctxT = [place(DK * TW).rearrange("p (k n) -> p k n", k=DK) for _ in range(2)]
        rest = [place(TW) for _ in range(2)]
        part1, part2, part3 = [[place(half).bitcast(BF16) for _ in range(G)] for _ in range(3)]
        vtile = [place(H * TC * VW).rearrange("p (h c w) -> p h c w", h=H, c=TC) for _ in range(2)]
        wk = place(DK * G * P).rearrange("p (k n) -> p k n", k=DK)
        wv = place(DK * D).rearrange("p (k n) -> p k n", k=DK)
        wq = place(DK * G * P).rearrange("p (k n) -> p k n", k=DK)
        bv_bc = place(D)
        qf, qrest = place(G * P), place(G * P)
        qpart = [place(G * P // 2).bitcast(BF16) for _ in range(3)]
        qzero = place(G * P // 2).bitcast(BF16)
        assert at[0] <= 2 * NT * TW, at

        kflat = kring[:, :].bitcast(FP32)
        w_in = view(kflat, 0, DK * 2 * DI).rearrange("p (k n) -> p k n", k=DK)
        w_out = view(kflat, DK * 2 * DI, CI * D).rearrange("p (k n) -> p k n", k=CI)
        vt = [0]

        def room(n):
            v = view(sflat, NT * TW + vt[0], n)
            vt[0] += n
            return v

        x1, x1n, x2, x2n, fin = room(D), room(D), room(D), room(D), room(D)
        x1nT = room(D).rearrange("p (k n) -> p k n", k=DK)
        x2nT = room(D).rearrange("p (k n) -> p k n", k=DK)
        attT = room(D).rearrange("p (k n) -> p k n", k=DK)
        xpad = room(CI * (P + TAPS)).rearrange("p (c n) -> p c n", c=CI)
        mark = vt[0]
        c4 = lambda: room(CI * P).rearrange("p (c n) -> p c n", c=CI)
        z_sb, conv, conv2, u, e1, e2, dt, sp, absd, keep, hs, y, bp, ub, sz = [c4() for _ in range(15)]
        xp = room(2 * P).rearrange("p (b n) -> p b n", b=2)
        FT = F1 // P
        assert vt[0] <= NT * TW
        vt[0] = mark
        f32h = [room(FT * P) for _ in range(2)]
        frest = room(FT * P)
        hp = [[room(FT * P // 2).bitcast(BF16) for _ in range(3)] for _ in range(3)]
        assert vt[0] <= NT * TW
        K0R, K1R, K2R = 2 * D // P, F1 // P, F1 // P
        w8n = (K0R * F1 + K1R * F1 + K2R * D) // 4
        w8 = view(sflat, 0, w8n).bitcast(U8)
        wbn = (K0R * F1 + K1R * F1 + K2R * D) // 2
        W8T = -(-w8n // TW)
        wb = view(sflat, W8T * TW, wbn).bitcast(BF16)
        assert W8T * TW + wbn <= NT * TW
        o1, o2 = K0R * F1, (K0R + K1R) * F1
        w0b = wb[:, 0:o1].rearrange("p (k n) -> p k n", k=K0R)
        w1b = wb[:, o1:o2].rearrange("p (k n) -> p k n", k=K1R)
        w2b = wb[:, o2:o2 + K2R * D].rearrange("p (k n) -> p k n", k=K2R)

        psA = [pb(f"psA{i}", [P, 2, 512]) for i in range(2)]
        psT = pb("psT", [P, 2, 512])
        psTf = psT[:, :, :].rearrange("p a n -> p (a n)")
        psO = pb("psO", [P, 512])
        psM = pb("psM", [P, 512])
        psH = (psO, psM)

        s_ld = sem("small_loads")
        s_x0 = sem("x_in")
        s_bkv = sem("key_value_biases_in")
        s_ctx = [sem(f"ctx_in{i}") for i in range(2)]
        s_wload = sem("weights_in")
        s_id = sem("identity_ready")
        s_one = sem("ones_ready")
        s_ln = sem("ln_chain")
        s_sq = sem("ln_sqrt")
        s_sv = sem("ln_var_ready")
        s_xn = sem("xn_ready")
        s_xt = sem("xn_transposed")
        s_xc = sem("xnT_ready")
        s_qm = sem("q_projected")
        s_qp = sem("q_parts_ready")
        s_qw = sem("q_rows_written")
        s_qs = sem("q_stack_loaded")
        s_tp = sem("ctx_transposed")
        s_ct = sem("ctxT_ready")
        s_kp = sem("key_projected")
        s_k1 = sem("key_part1_ready")
        s_r = sem("key_rest_ready")
        s_k2 = sem("key_part2_ready")
        s_k3 = sem("key_part3_ready")
        s_kw = [sem(f"key_rows_written{g}") for g in range(G)]
        s_vm = sem("values_projected")
        s_v = sem("values_ready")
        s_kin = [sem(f"key_tile_in{i}") for i in range(KRING)]
        s_mm = sem("scores_in_psum")
        s_cp = sem("scores_in_sbuf")
        s_exp = sem("exp_ready")
        s_msk = sem("masked_ready")
        s_t0 = sem("probsT_bank0")
        s_t1 = sem("probsT_bank1")
        s_e0 = sem("pt_from_scalar")
        s_e1 = sem("pt_from_vector")
        s_pv = sem("weighted_sum_added")
        s_vw = [sem(f"values_written{i}") for i in range(2)]
        s_vin = [sem(f"values_in{i}") for i in range(2)]
        s_max = sem("candidates_ready")
        s_lk = sem("threshold_chain")
        s_thr = sem("threshold_ready")
        s_fl = sem("flag_ready")
        s_fs = sem("flag_summed")
        s_fi = sem("flag_int_ready")
        s_gen = sem("general_path_chain")
        s_oev = sem("head_output_taken")
        s_w3 = sem("state_weights_in")
        s_w8 = sem("ffn_bytes_in")
        s_wb = sem("ffn_weights_ready")
        s_dv = sem("tail_vector_chain")
        T = {n: sem(n) for n in (
            "sums_done", "att_ready", "att_turned", "attT_ready", "wo_done", "var1", "std1", "x1n_ready", "x1n_turned", "x1nT_ready",
            "xc_done", "z_done", "conv_ready", "u_exp", "z_exp", "u_ready", "low_rank_done", "xp_ready", "dt_done",
            "bp_done", "abs_ready", "dt_exp", "dt_exp1", "dt_ln", "y_ready", "mix_done", "var2", "std2", "x2n_ready",
            "x2n_turned", "x2nT_ready", "in_parts", "ffn0_done", "h0_parts", "ffn1_done", "h1_parts", "ffn2_done",
            "z_taken", "output")}
        s_out = sem("output_written")

        block = ctx.enter_context(nc.Block())
        SMALL = 13

        def flat(v):
            return v.rearrange("p c n -> p (c n)")

        def scalar_tail(act):
            def wait(n):
                act.wait_ge(T[n], 1)

            def f(dst, src, func, done, **kw):
                nc.scalar.activation(dst, src, func, **kw).then_inc(T[done], 1)

            wait("att_turned")
            f(flat(attT), psM[:, 0:D], ACT.Copy, "attT_ready")
            wait("var1")
            f(rstd[:, 0:1], mv[:, 1:2], ACT.Sqrt, "std1")
            wait("x1n_turned")
            f(flat(x1nT), psM[:, 0:D], ACT.Copy, "x1nT_ready")
            wait("z_done")
            f(flat(z_sb), psA[1][:, 0, :], ACT.Copy, "z_taken")
            wait("z_taken")
            f(flat(e2), flat(z_sb), ACT.Exp, "z_exp", scale=-1.0)
            wait("conv_ready")
            f(flat(e1), flat(conv), ACT.Exp, "u_exp", scale=-1.0)
            wait("abs_ready")
            f(flat(sp), flat(absd), ACT.Exp, "dt_exp", scale=-1.0)
            wait("dt_exp1")
            f(flat(sp), flat(sp), ACT.Ln, "dt_ln")
            wait("var2")
            f(rstd[:, 0:1], mv[:, 1:2], ACT.Sqrt, "std2")
            wait("x2n_turned")
            f(flat(x2nT), psM[:, 0:D], ACT.Copy, "x2nT_ready")

        def tensor_tail(pe):
            def turn_rows(src, ready, done):
                pe.wait_ge(*ready)
                for k in range(DK):
                    last = nc.tensor.transpose(psM[:, k * P:(k + 1) * P], src[:, k * P:(k + 1) * P], ident[:, :])
                last.then_inc(T[done], 1)

            pe.wait_ge(s_oev, H + 2)
            for h in range(H):
                last = nc.tensor.matmul(psA[0][:, 0, h * VW:(h + 1) * VW], outT[:, h + 1, :], select[:, :],
                                        start=True, stop=True)
            last.then_inc(T["sums_done"], 1)
            turn_rows(att, (T["att_ready"], 1), "att_turned")
            pe.wait_ge(T["attT_ready"], 1)
            for k in range(DK):
                last = nc.tensor.matmul(psO[:, 0:D], attT[:, k, :], wo[:, k, :], start=(k == 0), stop=(k == DK - 1))
            last.then_inc(T["wo_done"], 1)
            turn_rows(x1n, (T["x1n_ready"], 1), "x1n_turned")
            pe.wait_ge(T["x1nT_ready"], 1)
            pe.wait_ge(s_w3, 32)
            for j, done in enumerate(("xc_done", "z_done")):
                for c in range(CI):
                    for k in range(DK):
                        col = j * DI + c * P
                        last = nc.tensor.matmul(psA[j][:, 0, c * P:(c + 1) * P], w_in[:, k, col:col + P], x1nT[:, k, :],
                                                start=(k == 0), stop=(k == DK - 1))
                last.then_inc(T[done], 1)
            pe.wait_ge(T["u_ready"], 1)
            for j in range(2):
                for c in range(CI):
                    last = nc.tensor.matmul(psM[0:DS, j * P:(j + 1) * P], wx[:, c, j * DS:(j + 1) * DS], u[:, c, :],
                                            start=(c == 0), stop=(c == CI - 1))
            last.then_inc(T["low_rank_done"], 1)
            pe.wait_ge(T["xp_ready"], 1)
            for j, (w, done) in enumerate(((wdt, "dt_done"), (wbp, "bp_done"))):
                for c in range(CI):
                    last = nc.tensor.matmul(psT[:, j, c * P:(c + 1) * P], w[:, c * P:(c + 1) * P], xp[0:DS, j, :],
                                            start=True, stop=True)
                last.then_inc(T[done], 1)
            pe.wait_ge(T["y_ready"], 1)
            for c in range(CI):
                last = nc.tensor.matmul(psO[:, 0:D], y[:, c, :], w_out[:, c, :], start=(c == 0), stop=(c == CI - 1))
            last.then_inc(T["mix_done"], 1)
            turn_rows(x2n, (T["x2n_ready"], 1), "x2n_turned")

            def layer(w, rows, parts, ps, done):
                for ft in range(F1 // P):
                    for k in range(rows):
                        for i in range(3):
                            last = nc.tensor.matmul(ps[:, ft // 4, (ft % 4) * P:(ft % 4 + 1) * P],
                                                    w[:, k, ft * P:(ft + 1) * P], parts[i][:, k * P:(k + 1) * P],
                                                    start=(k == 0 and i == 0), stop=(k == rows - 1 and i == 2))
                last.then_inc(T[done], 1)

            pe.wait_ge(s_wb, 1)
            pe.wait_ge(T["in_parts"], 1)
            layer(w0b, K0R, hp[0], psA[0], "ffn0_done")
            pe.wait_ge(s_wb, 3)
            pe.wait_ge(T["h0_parts"], 1)
            layer(w1b, K1R, hp[1], psA[1], "ffn1_done")
            pe.wait_ge(T["h1_parts"], 1)
            for k in range(K2R):
                for i in range(3):
                    last = nc.tensor.matmul(psO[:, 0:D], hp[2][i][:, k * P:(k + 1) * P], w2b[:, k, :],
                                            start=(k == 0 and i == 0), stop=(k == K2R - 1 and i == 2))
            last.then_inc(T["ffn2_done"], 1)

        def vector_tail(dve):
            cnt = [0]

            def link(ins):
                cnt[0] += 1
                ins.then_inc(s_dv, 1)
                dve.wait_ge(s_dv, cnt[0])

            def each(make):
                for c in range(CI):
                    cnt[0] += 1
                    make(c).then_inc(s_dv, 1)
                dve.wait_ge(s_dv, cnt[0])

            V = nc.vector

            def norm(src, dst, var, std, ready):
                link(V.bn_stats(stats[:, :], src))
                link(V.bn_aggr(mv[:, :], stats[:, :]))
                V.tensor_scalar(mv[:, 1:2], mv[:, 1:2], EPS, None, ALU.add).then_inc(T[var], 1)
                dve.wait_ge(T[std], 1)
                link(V.reciprocal(rstd[:, 1:2], rstd[:, 0:1]))
                V.tensor_scalar(dst, src, mv[:, 0:1], rstd[:, 1:2], ALU.subtract, ALU.mult).then_inc(T[ready], 1)

            link(V.memset(flat(xpad), 0.0))
            dve.wait_ge(T["sums_done"], 1)
            sums = psA[0][:, 0, 0:H * VW].rearrange("p (h w) -> p h w", w=VW)
            link(V.reciprocal(rsum[:, :], sums[:, :, DH:VW].rearrange("p h w -> p (h w)")))
            V.tensor_tensor(out=att[:, :].rearrange("p (h d) -> p h d", h=H), in0=sums[:, :, 0:DH],
                            in1=rsum[:, :].rearrange("p (h w) -> p h w", w=1).broadcast_to([P, H, DH]),
                            op=ALU.mult).then_inc(T["att_ready"], 1)
            dve.wait_ge(T["wo_done"], 1)
            link(V.tensor_tensor(out=x1, in0=psO[:, 0:D], in1=bo_bc[:, :], op=ALU.add))
            link(V.tensor_tensor(out=x1, in0=x1, in1=x0[:, :], op=ALU.add))
            norm(x1, x1n, "var1", "std1", "x1n_ready")
            dve.wait_ge(T["xc_done"], 1)
            link(V.tensor_copy(xpad[:, :, TAPS:], psA[0][:, 0, :].rearrange("p (c n) -> p c n", c=CI)))
            src = None
            for j in range(TAPS):
                dst = conv if j % 2 else conv2
                if j == 0:
                    each(lambda c: V.tensor_scalar(dst[:, c, :], xpad[:, c, 1:1 + P], cw[:, c, 0:1], None, ALU.mult))
                else:
                    each(lambda c: V.scalar_tensor_tensor(out=dst[:, c, :], in0=xpad[:, c, 1 + j:1 + j + P],
                                                          scalar=cw[:, c, j:j + 1], in1=src[:, c, :], op0=ALU.mult,
                                                          op1=ALU.add))
                src = dst
            V.engine_nop().then_inc(T["conv_ready"], 1)
            dve.wait_ge(T["u_exp"], 1)
            link(V.tensor_scalar(flat(e1), flat(e1), 1.0, None, ALU.add))
            link(V.reciprocal(flat(e1), flat(e1)))
            V.tensor_tensor(out=flat(u), in0=flat(conv), in1=flat(e1), op=ALU.mult).then_inc(T["u_ready"], 1)
            dve.wait_ge(T["z_exp"], 1)
            link(V.tensor_scalar(flat(e2), flat(e2), 1.0, None, ALU.add))
            link(V.reciprocal(flat(e2), flat(e2)))
            link(V.tensor_tensor(out=flat(sz), in0=flat(z_sb), in1=flat(e2), op=ALU.mult))
            dve.wait_ge(T["low_rank_done"], 1)
            V.tensor_copy(xp[0:DS, :, :], psM[0:DS, 0:2 * P].rearrange("p (b n) -> p b n", b=2))\
                .then_inc(T["xp_ready"], 1)
            dve.wait_ge(T["dt_done"], 1)
            each(lambda c: V.tensor_scalar(dt[:, c, :], psT[:, 0, c * P:(c + 1) * P], bdt[:, c:c + 1], None, ALU.add))
            link(V.tensor_scalar(flat(e1), flat(dt), -1.0, None, ALU.mult))
            V.tensor_tensor(out=flat(absd), in0=flat(dt), in1=flat(e1), op=ALU.max).then_inc(T["abs_ready"], 1)
            dve.wait_ge(T["bp_done"], 1)
            dve.wait_ge(T["u_ready"], 1)
            link(V.tensor_tensor(out=flat(ub), in0=psT[:, 1, :], in1=flat(u), op=ALU.mult))
            dve.wait_ge(T["dt_exp"], 1)
            V.tensor_scalar(flat(sp), flat(sp), 1.0, None, ALU.add).then_inc(T["dt_exp1"], 1)
            dve.wait_ge(T["dt_ln"], 1)
            link(V.scalar_tensor_tensor(out=flat(dt), in0=flat(dt), scalar=0.0, in1=flat(sp), op0=ALU.max,
                                        op1=ALU.add))
            link(V.tensor_scalar(flat(dt), flat(dt), 1e-4, 1.0, ALU.max, ALU.min))
            link(V.tensor_scalar(flat(keep), flat(dt), -1.0, 1.0, ALU.mult, ALU.add))
            each(lambda c: V.tensor_tensor_scan(hs[:, c, :], keep[:, c, :], ub[:, c, :], 0.0, ALU.mult, ALU.add))
            each(lambda c: V.scalar_tensor_tensor(out=y[:, c, :], in0=u[:, c, :], scalar=dpar[:, c:c + 1],
                                                  in1=hs[:, c, :], op0=ALU.mult, op1=ALU.add))
            V.tensor_tensor(out=flat(y), in0=flat(y), in1=flat(sz), op=ALU.mult).then_inc(T["y_ready"], 1)
            dve.wait_ge(T["mix_done"], 1)
            link(V.tensor_tensor(out=x2, in0=psO[:, 0:D], in1=x1, op=ALU.add))
            norm(x2, x2n, "var2", "std2", "x2n_ready")

            def parts(src, n, dst, r):
                link(V.tensor_copy(dst[0][:, 0:n], src))
                link(V.tensor_tensor(out=r, in0=src, in1=dst[0][:, 0:n], op=ALU.subtract))
                link(V.tensor_copy(dst[1][:, 0:n], r))
                link(V.tensor_tensor(out=dst[2][:, 0:n], in0=r, in1=dst[1][:, 0:n], op=ALU.subtract))

            dve.wait_ge(T["x2nT_ready"], 1)
            parts(flat(x2nT), D, hp[0], frest[:, 0:D])
            for i in range(3):
                link(V.tensor_scalar(hp[0][i][:, D:2 * D], hp[0][i][:, 0:D], -1.0, None, ALU.mult))
            V.engine_nop().then_inc(T["in_parts"], 1)
            for i, (ps, ready, done) in enumerate(((psA[0], "ffn0_done", "h0_parts"), (psA[1], "ffn1_done", "h1_parts"))):
                dve.wait_ge(T[ready], 1)
                psf = ps[:, :, :].rearrange("p a n -> p (a n)")
                link(V.tensor_scalar(f32h[i], psf, sc[:, i:i + 1], 0.0, ALU.mult, ALU.max))
                link(V.tensor_scalar(f32h[i], f32h[i], 2.0, None, ALU.mult))
                parts(f32h[i], F1, hp[i + 1], frest)
                V.engine_nop().then_inc(T[done], 1)
            dve.wait_ge(T["ffn2_done"], 1)
            V.scalar_tensor_tensor(out=fin, in0=psO[:, 0:D], scalar=sc[:, 2:3], in1=x2, op0=ALU.mult,
                                   op1=ALU.add).then_inc(T["output"], 1)

        @block.sync
        def _(sp):
            def load_ctx(t, i):
                src = a["ctx_1024"][0][bass.ds(t * TW, TW), :] if not isinstance(t, int) \
                    else a["ctx_1024"][0][t * TW:(t + 1) * TW, :]
                sp.dma_start(ctx_sb[i], src.rearrange("(c p) d -> p c d", p=P)).then_inc(s_ctx[i], 16)

            def weights(dst, name):
                sp.dma_start(dst, a[name].rearrange("(k p) n -> p k n", p=P)).then_inc(s_wload, 16)

            load_ctx(0, 0)
            weights(wk, "L0_xattn_Wk")
            weights(wv, "L0_xattn_Wv")
            load_ctx(1, 1)
            sp.dma_start(x0[:, :], a["x"][0]).then_inc(s_x0, 16)
            weights(wq, "L0_xattn_Wq")
            def key_writes(t, last=False):
                for g in range(G):
                    u = G * t + g
                    cols = bass.ds(t * TW, TW)
                    rows = slice(g * P, (g + 1) * P)
                    sp.wait_ge(s_k1, u + 1)
                    sp.dma_start(key_parts[rows, 0, cols], part1[g]).then_inc(s_kw[g], 16)
                    sp.dma_start(key_parts[rows, 3, cols], part1[g]).then_inc(s_kw[g], 16)
                    sp.wait_ge(s_k2, u + 1)
                    sp.dma_start(key_parts[rows, 1, cols], part2[g]).then_inc(s_kw[g], 16)
                    sp.wait_ge(s_k3, u + 1)
                    sp.dma_start(key_parts[rows, 2, cols], part3[g]).then_inc(s_kw[g], 16)

            def value_writes(t, i):
                sp.wait_ge(s_v, TC * (t + 1))
                sp.dma_start(value_rows[:, :, bass.ds(t * TC * VW, TC * VW)].rearrange("h p n -> p h n"),
                             vtile[i].rearrange("p h c w -> p h (c w)")).then_inc(s_vw[i], 16)

            for t in range(2):
                sp.wait_ge(s_tp, 2 * (t + 1))
                load_ctx(t + 2, t)
                key_writes(t)
                value_writes(t, t)
            sp.wait_ge(s_qp, 2)
            places = {(0, 0): 0, (1, 0): 0, (2, 0): 0, (3, 0): 1, (0, 1): 2, (1, 1): 1, (2, 1): 1, (3, 1): 3}
            for (s, b), i in places.items():
                src = (qpart + [qzero])[i].rearrange("p (g q) -> p g q", g=G)
                sp.dma_start(qry_parts[:, :, s, b, :], src).then_inc(s_qw, 16)

            with sp.Fori(1, NT // 2 - 1) as i:
                for j in range(2):
                    sp.wait_ge(s_tp, 2 * (2 * i + j + 1))
                    load_ctx(2 * i + j + 2, j)
                    key_writes(2 * i + j)
                    value_writes(2 * i + j, j)
            for t in range(NT - 2, NT):
                key_writes(t)
                value_writes(t, t % 2)
            for g in range(G):
                sp.wait_ge(s_kw[g], 4 * 16 * NT)

            sp.wait_ge(s_qw, 16 * len(places))
            sp.dma_start(qstack[:, :, :, :], qry_rows.rearrange("(h p) b q -> p h b q", p=P)).then_inc(s_qs, 16)

            def stream(h, t):
                sp.dma_start(kring[:, (t % KRING) * TW:(t % KRING + 1) * TW],
                             key_rows[bass.ds(h * P, P), t * TW:(t + 1) * TW]).then_inc(s_kin[t % KRING], 16)

            for t in range(KRING):
                stream(0, t)
            for t in range(KRING, NT):
                sp.wait_ge(s_mm, t - KRING + 1)
                stream(0, t)
            with sp.Fori(1, H) as h:
                for t in range(NT):
                    sp.wait_ge(s_mm, h * NT + (t - KRING + 1))
                    stream(h, t)
            sp.wait_ge(s_mm, H * NT)
            sp.dma_start(w_in, a["L0_attn_W_in"].rearrange("(k p) n -> p k n", p=P)).then_inc(s_w3, 16)
            sp.dma_start(w_out, a["L0_attn_W_out"].rearrange("(k p) n -> p k n", p=P)).then_inc(s_w3, 16)
            sp.wait_ge(s_msk, (H - 2) * NT + W8T)
            for k, lo, rows, n in (("L0_ffn_k0", 0, K0R, F1), ("L0_ffn_k1", o1, K1R, F1), ("L0_ffn_k2", o2, K2R, D)):
                sp.dma_start(w8[:, lo:lo + rows * n].rearrange("p (k n) -> p k n", k=rows),
                             a[k].rearrange("(k p) n -> p k n", p=P)).then_inc(s_w8, 16)
            sp.wait_ge(T["output"], 1)
            sp.dma_start(out[0], fin).then_inc(s_out, 16)
            sp.wait_ge(s_out, 16)

        @block.gpsimd
        def _(pool):
            nc.gpsimd.memset(ident[:, :], 0.0).then_inc(s_id, 1)
            nc.gpsimd.memset(ones[:, :], 1.0).then_inc(s_one, 1)
            pool.wait_ge(s_id, 1)
            nc.gpsimd.affine_select(out=ident[:, :], in_=ident[:, :], compare_op=ALU.not_equal, fill=1.0, base=0,
                                    pattern=[[-1, P]], channel_multiplier=1).then_inc(s_id, 1)
            for i in range(2):
                nc.gpsimd.memset(vtile[i][:, :, :, DH:VW], 1.0).then_inc(s_one, 1)

            def third_part(t, g):
                pool.wait_ge(s_k2, G * t + g + 1)
                if not (isinstance(t, int) and t == 0):
                    pool.wait_ge(s_kw[g], 64 * t)
                nc.gpsimd.tensor_tensor(out=part3[g], in0=rest[g % 2], in1=part2[g],
                                        op=ALU.subtract).then_inc(s_k3, 1)

            for g in range(G):
                third_part(0, g)
            with pool.Fori(1, NT) as t:
                for g in range(G):
                    third_part(t, g)
            for i in range(2):
                pool.wait_ge(s_vw[i], 16 * NT // 2)
            for i in range(2):
                pool.dma_start(vhead[:, i, :, :].rearrange("p c w -> p (c w)"), value_rows[i]).then_inc(s_vin[i], 16)
            with pool.Fori(0, (H - 2) // 2) as i:
                for j in range(2):
                    pool.wait_ge(s_pv, (2 * i + j + 1) * NT + 2)
                    pool.dma_start(vhead[:, j, :, :].rearrange("p c w -> p (c w)"),
                                   value_rows[bass.ds(2 * i + j + 2, 1)].rearrange("o p n -> (o p) n"))\
                        .then_inc(s_vin[j], 16)
            pool.wait_ge(s_w8, 48)
            pool.wait_ge(s_msk, (H - 1) * NT)
            for lo, n in ((0, o1), (o1, o2 - o1), (o2, K2R * D)):
                nc.gpsimd.tensor_scalar(wb[:, lo:lo + n], w8[:, lo:lo + n], 2.0, -1.0, ALU.mult,
                                        ALU.add).then_inc(s_wb, 1)

        @block.scalar
        def _(act):
            def bcast(dst, src, n, done=s_ld):
                act.dma_start(dst, src.rearrange("(o n) -> o n", o=1).broadcast_to([P, n])).then_inc(done, 16)

            def cols(dst, src, done=s_ld):
                act.dma_start(dst, src.rearrange("(g p) -> p g", p=P), allow_slow_non_contiguous=True)\
                    .then_inc(done, 16)

            cols(bk[:, :], a["L0_xattn_bk"], s_bkv)
            bcast(bv_bc, a["L0_xattn_bv"], D, s_bkv)
            cols(bq[:, :], a["L0_xattn_bq"])
            bcast(bo_bc[:, :], a["L0_xattn_bo"], D)
            bcast(pos[:, :], a["L0_xattn_pos_bias"].rearrange("a h b c -> (a h b c)"), H)
            act.dma_start(wo[:, :, :], a["L0_xattn_Wo"].rearrange("(k p) n -> p k n", p=P)).then_inc(s_ld, 16)
            act.dma_start(cw[:, :, :], a["L0_attn_conv_w"].rearrange("(c p) o k -> p c (o k)", p=P)).then_inc(s_ld, 16)
            act.dma_start(wx[:, :, :], a["L0_attn_W_x"].rearrange("(c p) n -> p c n", p=P)).then_inc(s_ld, 16)
            act.dma_start(wdt[:, :], a["L0_attn_W_dt"]).then_inc(s_ld, 16)
            act.dma_start(wbp[:, :], a["L0_attn_W_Bp"]).then_inc(s_ld, 16)
            cols(bdt[:, :], a["L0_attn_b_dt"])
            cols(dpar[:, :], a["L0_attn_D_param"])
            for i in range(3):
                bcast(sc[:, i:i + 1], a[f"L0_ffn_s{i}"], 1)
            act.wait_ge(s_sv, 1)
            nc.scalar.activation(rstd[:, 0:1], mv[:, 1:2], ACT.Sqrt).then_inc(s_sq, 1)
            act.wait_ge(s_bkv, 32)

            def take_ctxT(t, i, k):
                act.wait_ge(s_tp, 2 * t + k + 1)
                if k == 0:
                    act.wait_ge(s_vm, TC * t)
                nc.scalar.activation(ctxT[i][:, k, :], psTf[:, 0:TW], ACT.Copy).then_inc(s_ct, 1)

            def take_part1(t, g):
                u = G * t + g
                act.wait_ge(s_kp, u + 1)
                if not (isinstance(t, int) and t == 0):
                    act.wait_ge(s_kw[g], 64 * t)
                nc.scalar.activation(part1[g].rearrange("p (a n) -> p a n", a=2), psA[g % 2][:, :, 0:HW],
                                     ACT.Identity, bias=bk[:, g:g + 1]).then_inc(s_k1, 1)

            def take_part2(t, g):
                act.wait_ge(s_r, G * t + g + 3)
                nc.scalar.activation(part2[g], rest[g % 2], ACT.Copy).then_inc(s_k2, 1)

            def key_tile(t, i, more):
                if more:
                    take_ctxT(t + 1, 1 - i, 0)
                take_part1(t, 0)
                if more:
                    take_ctxT(t + 1, 1 - i, 1)
                for g in range(1, G):
                    take_part1(t, g)
                    take_part2(t, g - 1)
                take_part2(t, G - 1)

            take_ctxT(0, 0, 0)
            take_ctxT(0, 0, 1)
            for t in range(2):
                key_tile(t, t, True)
            act.wait_ge(s_xt, 1)
            nc.scalar.activation(xnT[:, :, :], psM[:, 0:D].rearrange("p (k n) -> p k n", k=DK),
                                 ACT.Copy).then_inc(s_xc, 1)
            with act.Fori(1, NT // 2 - 1) as i:
                for j in range(2):
                    key_tile(2 * i + j, j, True)
            key_tile(NT - 2, 0, True)
            key_tile(NT - 1, 1, False)

            def copy_scores(hA, par, t):
                n = hA * NT + t
                act.wait_ge(s_mm, n + 1)
                if not (isinstance(hA, int) and hA < 2):
                    act.wait_ge(s_msk, n - 2 * NT + 1)
                elif t == 0:
                    act.wait_ge(s_vm, TC * (NT + 1))
                    act.wait_ge(s_v, TC * NT)
                    for g in range(G):
                        act.wait_ge(s_kw[g], 64 * NT)
                    for i in range(2):
                        act.wait_ge(s_vw[i], 8 * NT)
                nc.scalar.activation(scores2[:, par, t * TW:(t + 1) * TW].rearrange("p (a n) -> p a n", a=2),
                                     psA[t % 2][:, :, 0:HW], ACT.Copy).then_inc(s_cp, 1)

            def exps(hB, par, t):
                m = hB * NT + t
                if t == 0:
                    act.wait_ge(s_thr, hB + 1)
                act.wait_ge(s_t1, m + 1)
                nc.scalar.activation(probs[:, t % 2, :], scores2[:, par, t * TW:(t + 1) * TW], ACT.Exp,
                                     bias=nbias[:, par:par + 1]).then_inc(s_exp, 1)

            def take_pt(hB, t, helped):
                m = hB * NT + t
                act.wait_ge(s_pv, m + 1)
                if helped:
                    act.wait_ge(s_t0, m + 1)
                    nc.scalar.activation(pt[:, t % 2, 0:C0 * P], psT[:, 0, 0:C0 * P], ACT.Copy).then_inc(s_e0, 1)
                else:
                    act.wait_ge(s_t1, m + 3)
                    nc.scalar.activation(pt[:, t % 2, :], psTf[:, 0:TW], ACT.Copy).then_inc(s_e0, 1)

            def head(hB, hA, par, more=True):
                for t in range(NT):
                    if hB is not None and t + 1 < NT:
                        exps(hB, par, t + 1)
                    elif hB is not None and more:
                        exps(hB + 1, 1 - par, 0)
                    if hA is not None:
                        copy_scores(hA, par, t)
                    if hB is not None:
                        take_pt(hB, t, hA is None)

            for par in range(2):
                head(None, par, par)
            exps(0, 0, 0)
            with act.Fori(0, H // 2 - 1) as i:
                for par in range(2):
                    head(2 * i + par, 2 * i + par + 2, par)
            head(H - 2, None, 0)
            head(H - 1, None, 1, more=False)
            scalar_tail(act)

        @block.tensor
        def _(pe):
            pe.sem_inc(s_vm, TC)
            pe.sem_inc(s_t1, 2)
            pe.sem_inc(s_pv, 2)
            pe.sem_inc(s_e0, 1)
            pe.sem_inc(s_oev, 1)
            pe.wait_ge(s_id, 2)

            def project_queries():
                pe.wait_ge(s_xn, 1)
                pe.wait_ge(s_v, 2 * TC)
                for k in range(DK):
                    last = nc.tensor.transpose(psM[:, k * P:(k + 1) * P], xn[:, k * P:(k + 1) * P], ident[:, :])
                last.then_inc(s_xt, 1)
                pe.wait_ge(s_xc, 1)
                for g in range(G):
                    for k in range(DK):
                        last = nc.tensor.matmul(psO[:, g * P:(g + 1) * P], wq[:, k, g * P:(g + 1) * P], xnT[:, k, :],
                                                start=(k == 0), stop=(k == DK - 1))
                last.then_inc(s_qm, 1)

            def turn_ctx(t, i, k):
                if k == 0:
                    n = (t // 2 + 1) if isinstance(t, int) else None
                    pe.wait_ge(s_ctx[i], 16 * n if n is not None else 8 * (t - i) + 16)
                pe.wait_ge(s_ct, 2 * t + k)
                for c in range(TC):
                    last = nc.tensor.transpose(psTf[:, c * P:(c + 1) * P], ctx_sb[i][:, c, k * P:(k + 1) * P],
                                               ident[:, :])
                last.then_inc(s_tp, 1)

            def project_keys(t, i, g):
                if g == 0:
                    pe.wait_ge(s_ct, 2 * t + 2)
                pe.wait_ge(s_r, G * t + g + 1)
                for a_ in range(2):
                    for k in range(DK):
                        last = nc.tensor.matmul(psA[g % 2][:, a_, 0:HW], wk[:, k, g * P:(g + 1) * P],
                                                ctxT[i][:, k, a_ * HW:(a_ + 1) * HW],
                                                start=(k == 0), stop=(k == DK - 1))
                last.then_inc(s_kp, 1)

            def project_values(t, i):
                if not (isinstance(t, int) and t < 2):
                    pe.wait_ge(s_qp, 2)
                for c in range(TC):
                    w = TC * t + c
                    bank = (psO, psM)[c % 2]
                    if c == 0 and not (isinstance(w, int) and w == 0):
                        pe.wait_ge(s_v, w)
                    elif c > 1:
                        pe.wait_ge(s_v, w - 1)
                    for k in range(DK):
                        last = nc.tensor.matmul(bank[:, 0:D], ctxT[i][:, k, c * P:(c + 1) * P], wv[:, k, :],
                                                start=(k == 0), stop=(k == DK - 1))
                    last.then_inc(s_vm, 1)

            def key_tile(t, i, more):
                if more:
                    turn_ctx(t + 1, 1 - i, 0)
                project_keys(t, i, 0)
                if more:
                    turn_ctx(t + 1, 1 - i, 1)
                for g in range(1, G):
                    project_keys(t, i, g)
                project_values(t, i)

            turn_ctx(0, 0, 0)
            turn_ctx(0, 0, 1)
            pe.wait_ge(s_wload, 48)
            for t in range(2):
                key_tile(t, t, True)
            project_queries()
            with pe.Fori(1, NT // 2 - 1) as i:
                for j in range(2):
                    key_tile(2 * i + j, j, True)
            key_tile(NT - 2, 0, True)
            key_tile(NT - 1, 1, False)

            def score_tile(hA, t):
                n = hA * NT + t
                pe.wait_ge(s_kin[t % KRING], 16 * (2 * hA + t // KRING + 1))
                if not (isinstance(hA, int) and n < 2):
                    pe.wait_ge(s_cp, n - 1)
                for a_ in range(2):
                    cols = kring[:, (t % KRING) * TW + a_ * HW:(t % KRING) * TW + (a_ + 1) * HW]
                    for b in range(2):
                        lhsT = qstack[:, hA, b, :] if isinstance(hA, int) else qstack[:, bass.ds(hA, 1), b, :]\
                            .rearrange("p o q -> p (o q)")
                        last = nc.tensor.matmul(psA[t % 2][:, a_, 0:HW], lhsT, cols, start=(b == 0), stop=(b == 1))
                last.then_inc(s_mm, 1)

            def turn(hB, t):
                m = hB * NT + t
                pe.wait_ge(s_msk, m + 1)
                pe.wait_ge(s_e0, m + 1)
                if isinstance(hB, int) and hB >= H - 2 and m > (H - 2) * NT:
                    pe.wait_ge(s_e1, m - (H - 2) * NT)
                for c in range(TC):
                    last = nc.tensor.transpose(psTf[:, c * P:(c + 1) * P], probs[:, t % 2, c * P:(c + 1) * P],
                                               ident[:, :])
                    if c == C0 - 1:
                        last.then_inc(s_t0, 1)
                last.then_inc(s_t1, 1)

            def weigh(hB, par, t):
                m = hB * NT + t
                pe.wait_ge(s_e0, m + 2)
                if isinstance(hB, int) and hB >= H - 2:
                    pe.wait_ge(s_e1, m - (H - 2) * NT + 1)
                if t == 0:
                    pe.wait_ge(s_oev, hB + 1)
                    pe.wait_ge(s_vin[par], 16 * (hB + 2 - par) // 2 if isinstance(hB, int) else 8 * (hB + 2 - par))
                for c in range(TC):
                    q = c % NQ
                    last = nc.tensor.matmul(psH[par][QUAD * q:QUAD * q + VW, 0:P], vhead[:, par, t * TC + c, :],
                                            pt[:, t % 2, c * P:(c + 1) * P], start=(t == 0 and c < NQ),
                                            stop=(t == NT - 1 and c >= TC - NQ))
                last.then_inc(s_pv, 1)

            def sum_flags(hT, par):
                pe.wait_ge(s_fl, hT + 1)
                nc.tensor.matmul(psH[par][0:1, 2 * P:2 * P + 1], flag[:, 0:1], ones[:, :], start=True, stop=True)\
                    .then_inc(s_fs, 1)

            def head(hB, hA, hT, par, more=True):
                for t in range(NT):
                    if hB is not None:
                        turn(hB, t)
                    if hA is not None and t + 1 < NT:
                        score_tile(hA, t + 1)
                    elif hA is not None and more:
                        score_tile(hA + 1, 0)
                    if hB is not None and t > 0:
                        weigh(hB, par, t - 1)
                    if hT is not None and t == FLAG_T:
                        sum_flags(hT, 1 - par)
                if hB is not None:
                    weigh(hB, par, NT - 1)

            pe.wait_ge(s_v, TC * NT)
            pe.wait_ge(s_qs, 16)
            score_tile(0, 0)
            head(None, 0, None, 0)
            head(None, 1, 0, 1)
            with pe.Fori(0, H // 2 - 2) as i:
                for par in range(2):
                    head(2 * i + par, 2 * i + par + 2, 2 * i + par + 1, par)
            head(H - 4, H - 2, H - 3, 0)
            head(H - 3, H - 1, H - 2, 1, more=False)
            head(H - 2, None, H - 1, 0)
            head(H - 1, None, None, 1)
            tensor_tail(pe)

        @block.vector
        def _(dve):
            dve.sem_inc(s_r, 2)
            n_ln = [0]

            def link(ins):
                n_ln[0] += 1
                ins.then_inc(s_ln, 1)
                dve.wait_ge(s_ln, n_ln[0])

            dve.wait_ge(s_x0, 16)
            link(nc.vector.bn_stats(stats[:, :], x0[:, :]))
            link(nc.vector.bn_aggr(mv[:, :], stats[:, :]))
            nc.vector.tensor_scalar(mv[:, 1:2], mv[:, 1:2], EPS, None, ALU.add).then_inc(s_sv, 1)
            dve.wait_ge(s_sq, 1)
            link(nc.vector.reciprocal(rstd[:, 1:2], rstd[:, 0:1]))
            nc.vector.tensor_scalar(xn[:, :], x0[:, :], mv[:, 0:1], rstd[:, 1:2], ALU.subtract,
                                    ALU.mult).then_inc(s_xn, 1)
            dve.wait_ge(s_one, 3)
            dve.wait_ge(s_bkv, 32)

            def query_parts():
                dve.wait_ge(s_ld, 16 * SMALL)
                dve.wait_ge(s_qm, 1)
                for g in range(G):
                    link(nc.vector.tensor_scalar(qf[:, g * P:(g + 1) * P], psO[:, g * P:(g + 1) * P], bq[:, g:g + 1],
                                                 1.0 / math.sqrt(R), ALU.add, ALU.mult))
                link(nc.vector.tensor_copy(qpart[0], qf))
                link(nc.vector.tensor_tensor(out=qrest, in0=qf, in1=qpart[0], op=ALU.subtract))
                link(nc.vector.tensor_copy(qpart[1], qrest))
                nc.vector.tensor_tensor(out=qpart[2], in0=qrest, in1=qpart[1], op=ALU.subtract).then_inc(s_qp, 1)
                nc.vector.memset(qzero, 0.0).then_inc(s_qp, 1)
                dve.wait_ge(s_id, 2)
                link(nc.vector.tensor_tensor(out=select[:, :], in0=ident[:, 0:VW], in1=ident[:, QUAD:QUAD + VW],
                                             op=ALU.add))
                for q in range(2, NQ):
                    link(nc.vector.tensor_tensor(out=select[:, :], in0=select[:, :],
                                                 in1=ident[:, QUAD * q:QUAD * q + VW], op=ALU.add))

            def key_tile(t, i):
                for g in range(G):
                    u = G * t + g
                    dve.wait_ge(s_k1, u + 1)
                    if not (isinstance(t, int) and u < 2):
                        dve.wait_ge(s_k3, u - 1)
                    nc.vector.scalar_tensor_tensor(
                        out=rest[g % 2].rearrange("p (a n) -> p a n", a=2), in0=psA[g % 2][:, :, 0:HW],
                        scalar=bk[:, g:g + 1], in1=part1[g].rearrange("p (a n) -> p a n", a=2),
                        op0=ALU.add, op1=ALU.subtract).then_inc(s_r, 1)
                for c in range(TC):
                    w = TC * t + c
                    dve.wait_ge(s_vm, w + 1 + TC)
                    if c == 0 and not (isinstance(t, int) and t < 2):
                        dve.wait_ge(s_vw[i], 8 * (t - i))
                    nc.vector.tensor_tensor(out=vtile[i][:, :, c, 0:DH], in0=(psO, psM)[c % 2][:, 0:D].rearrange("p (h d) -> p h d", h=H),
                                            in1=bv_bc.rearrange("p (h d) -> p h d", h=H), op=ALU.add)\
                        .then_inc(s_v, 1)

            for t in range(2):
                key_tile(t, t)
            query_parts()
            with dve.Fori(1, NT // 2) as i:
                for j in range(2):
                    key_tile(2 * i + j, j)

            def mask(hB, par, t):
                m = hB * NT + t
                dve.wait_ge(s_exp, m + 1)
                nc.vector.scalar_tensor_tensor(out=probs[:, t % 2, :], in0=scores2[:, par, t * TW:(t + 1) * TW],
                                               scalar=thr[:, par:par + 1], in1=probs[:, t % 2, :], op0=ALU.is_ge,
                                               op1=ALU.mult).then_inc(s_msk, 1)

            def take_candidates(hA, par, t):
                n = hA * NT + t
                dve.wait_ge(s_cp, n + 1)
                dve.nop(nofuse=True)
                for j in range(NSUB):
                    i = t * NSUB + j
                    last = nc.vector.max(cand[:, par, 8 * i:8 * i + 8],
                                         scores2[:, par, t * TW + j * SUB:t * TW + (j + 1) * SUB])
                last.then_inc(s_max, 1)

            def help_pt(hB, t):
                m = hB * NT + t
                dve.wait_ge(s_t1, m + 3)
                dve.wait_ge(s_pv, m + 1)
                nc.vector.tensor_copy(pt[:, t % 2, C0 * P:TW], psT[:, 1, 0:TW - C0 * P]).then_inc(s_e1, 1)

            def threshold_steps(hT, par):
                c = cand[:, par, :]
                step = [0]

                def done():
                    dve.wait_ge(s_lk, hT * LINKS + step[0])
                    dve.nop(nofuse=True)

                def count(ins):
                    step[0] += 1
                    ins.then_inc(s_lk, 1)

                def bound():
                    dve.wait_ge(s_max, (hT + 1) * NT)
                    count(nc.vector.tensor_reduce(flag[:, 1:2], c.rearrange("p (s e) -> p s e", e=8)[:, :, 7:8]
                                                  .rearrange("p s e -> p (s e)"), AX.X, ALU.max))

                def largest(r):
                    done()
                    count(nc.vector.max(top[:, 8 * r:8 * r + 8], c))

                def remove(r):
                    done()
                    count(nc.vector.match_replace(c, top[:, 8 * r:8 * r + 8], c, NEG))

                def raise_flag():
                    dve.wait_ge(s_lk, hT * LINKS + step[0])
                    nc.vector.tensor_tensor(out=flag[:, 0:1], in0=flag[:, 1:2], in1=top[:, TOPK - 1:TOPK],
                                            op=ALU.is_ge).then_inc(s_fl, 1)

                def read_flag():
                    dve.wait_ge(s_fs, hT + 1)
                    nc.vector.tensor_copy(flag_i[:, :], psH[par][0:1, 2 * P:2 * P + 1]).then_inc(s_fi, 1)

                def finish():
                    dve.wait_ge(s_fi, hT + 1)
                    dve.nop(nofuse=True)
                    flagged = dve.value_load(flag_i[0:1, 0:1], min_val=0, max_val=P)
                    with dve.If(flagged > 0):
                        general_threshold(par)
                    pcol = pos[:, hT:hT + 1] if isinstance(hT, int) else pos[:, bass.ds(hT, 1)]
                    count(nc.vector.tensor_copy(thr[:, par:par + 1], top[:, TOPK - 1:TOPK]))
                    count(nc.vector.tensor_tensor(out=rowmax[:, 0:1], in0=top[:, 0:1], in1=pcol, op=ALU.add))
                    dve.wait_ge(s_lk, hT * LINKS + step[0])
                    assert step[0] == LINKS - 1, step[0]
                    nc.vector.tensor_tensor(out=nbias[:, par:par + 1], in0=pcol, in1=rowmax[:, 0:1],
                                            op=ALU.subtract).then_inc(s_lk, 1)
                    dve.wait_ge(s_lk, (hT + 1) * LINKS)
                    dve.sem_inc(s_thr, 1)

                steps = [bound]
                for r in range(TOPK // 8):
                    steps.append(lambda r=r: largest(r))
                    if r + 1 < TOPK // 8:
                        steps.append(lambda r=r: remove(r))
                steps.append(raise_flag)
                assert len(steps) == FLAG_T - 1
                return steps, read_flag, finish

            def general_threshold(par):
                cnt = [0]

                def chain(ins):
                    cnt[0] += 1
                    ins.then_inc(s_gen, 1)
                    dve.wait_ge(s_gen, cnt[0])

                def fold(src):
                    chain(nc.vector.tensor_copy(merge[:, TOPK:TOPK + SUB], src))
                    for r in range(TOPK // 8):
                        chain(nc.vector.max(top[:, 8 * r:8 * r + 8], merge[:, :]))
                        chain(nc.vector.match_replace(merge[:, :], top[:, 8 * r:8 * r + 8], merge[:, :], NEG))
                    chain(nc.vector.tensor_copy(merge[:, 0:TOPK], top[:, :]))
                    dve.sem_clear(s_gen)
                    cnt[0] = 0

                chain(nc.vector.memset(merge[:, 0:TOPK], NEG))
                dve.sem_clear(s_gen)
                cnt[0] = 0
                with dve.Fori(0, NT * NSUB) as i:
                    fold(scores2[:, par, bass.ds(i * SUB, SUB)])

            def take_output(hO, par):
                dve.wait_ge(s_pv, hO * NT + 2)
                dst = outT[:, hO, :] if isinstance(hO, int) else \
                    outT[:, bass.ds(hO, 1), :].rearrange("p o q -> p (o q)")
                nc.vector.tensor_copy(dst, psH[par][:, 0:P]).then_inc(s_oev, 1)

            def head(hB, hA, hT, par):
                steps, read_flag, finish = threshold_steps(hT, 1 - par) if hT is not None else ([], None, None)
                for t in range(NT):
                    if hB is not None:
                        mask(hB, par, t)
                        if t == 1:
                            take_output(hB, 1 - par)
                    if t > 0 and hA is not None:
                        take_candidates(hA, par, t - 1)
                    elif t == 0 and hT is not None:
                        take_candidates(hT, 1 - par, NT - 1)
                    if 0 < t <= len(steps):
                        steps[t - 1]()
                    if hT is not None and t == FLAG_T + 1:
                        read_flag()
                    if hT is not None and t == FLAG_T + 2:
                        finish()
                    if hB is not None and hA is None:
                        help_pt(hB, t)

            head(None, 0, None, 0)
            head(None, 1, 0, 1)
            with dve.Fori(0, H // 2 - 1) as i:
                for par in range(2):
                    head(2 * i + par, 2 * i + par + 2, 2 * i + par + 1, par)
            head(H - 2, None, H - 1, 0)
            head(H - 1, None, None, 1)
            take_output(H, 1)
            vector_tail(dve)


def kernel(**inputs):
    import numpy as _np
    import concourse.bacc as _bacc
    from concourse import mybir as _mybir
    from concourse.bass_utils import run_bass_kernel_spmd as _run

    nc = _bacc.Bacc("TRN2", target_bir_lowering=False, num_devices=1)
    arrays, handles = {}, {}
    for name, value in inputs.items():
        v = _np.ascontiguousarray(value)
        if v.ndim == 0:
            v = v.reshape(1)
        arrays[f"in_{name}"] = v
        handles[name] = nc.dram_tensor(f"in_{name}", v.shape, _mybir.dt.from_np(v.dtype), kind="ExternalInput").ap()
    out = nc.dram_tensor("out_0", (1, P, D), _mybir.dt.float32, kind="ExternalOutput").ap()
    perceiver_block(nc, handles, out)
    r = _run(nc, [arrays], core_ids=[0])
    return r.results[0]["out_0"]
```

```python
import math
from contextlib import ExitStack

import concourse.bass as bass
from concourse import mybir

FP32 = mybir.dt.float32
BF16 = mybir.dt.bfloat16
F32R = mybir.dt.float32r
U8 = mybir.dt.uint8
I32 = mybir.dt.int32
ACT = mybir.ActivationFunctionType
ALU = mybir.AluOpType
AX = mybir.AxisListType

P = 128
D = 256
DK = D // P
H = 16
R = 32
DH = D // H
VW = DH + 1
VT = 128
TOPK = 32
S_LEN = 12544
TC = 7
TW = TC * P
HW = TW // 2
NT = S_LEN // TW
SUB = HW // 2
NSUB = TW // SUB
G = H * R // P
NPART = 3
RP = R * NPART
TURN_G = 2
C0 = 4
KRING = 7
QUAD = 32
NQ = P // QUAD
DI = 512
DS = 16
CI = DI // P
TAPS = 4
F1 = 1024
NEG = -3.0e38
EPS = 1e-5
LINKS = 11
FLAG_T = 9


def perceiver_block(nc, a, out):
    ctx = ExitStack()
    with ctx:
        def sb(name, shape, dt=FP32):
            return ctx.enter_context(nc.sbuf_tensor(name, shape, dt))

        def pb(name, shape):
            return ctx.enter_context(nc.psum_tensor(name, shape, FP32))

        def sem(name):
            return ctx.enter_context(nc.semaphore(name))

        key_rows = nc.dram_tensor("key_rows", (H * RP, S_LEN), BF16, kind="Internal").ap()
        key_parts = key_rows.rearrange("(n s) c -> n s c", s=NPART)
        qry_rows = nc.dram_tensor("qry_rows", (H * RP, 2, P), BF16, kind="Internal").ap()
        qry_again = nc.dram_tensor("qry_again", (H * R, 2, P), BF16, kind="Internal").ap()
        qry_parts = qry_rows.rearrange("(g p s) b q -> p g s b q", g=G, s=NPART)
        qry_fourth = qry_again.rearrange("(g p) b q -> p g b q", g=G)
        value_rows = nc.dram_tensor("value_rows", (H, P, NT * VT), FP32, kind="Internal").ap()

        def sb_below(name, shape, dt):
            with nc.sbuf_tensor(name, shape, dt) as tensor:
                return tensor

        ctx_split = sb_below("ctx_split", [P, 2, 2, DK, TW], F32R)
        scores2 = sb("scores", [P, 2, NT * TW])
        wkv_split = sb_below("wkv_split", [P, 2, DK * (G * P + D)], F32R)
        vhead = sb("vhead", [P, 2, NT, VT])
        outT = sb("outT", [P, H + 1, P])
        select = sb("select", [P, VW])
        kring = sb("kring", [P, KRING * TW], BF16)
        probs = sb("probs", [P, 4, TW])
        pt = sb("pt", [P, 2, TW])
        qstack = sb("qstack", [P, H, 2, P], BF16)
        cand = sb("cand", [P, 2, NT * NSUB * 8])
        merge = sb("merge", [P, TOPK + SUB])
        top = sb("top", [P, TOPK])
        x0 = sb("x0", [P, D])
        xn = sb("xn", [P, D])
        xnT = sb("xnT", [P, DK, P])
        att = sb("att", [P, D])
        wo = sb("wo", [P, DK, D])
        bo_bc = sb("bo_bc", [P, D])
        ident = sb("ident", [P, P])
        stats = sb("stats", [P, 6])
        mv = sb("mv", [P, 2])
        rstd = sb("rstd", [P, 2])
        bq = sb("bq", [P, G])
        bk = sb("bk", [P, G])
        pos = sb("pos", [P, H])
        nbias = sb("nbias", [P, 2])
        thr = sb("thr", [P, 2])
        rowmax = sb("rowmax", [P, 2])
        flag = sb("flag", [P, 2])
        flag_i = sb("flag_i", [1, 1], I32)
        ones = sb("ones", [P, 1])
        rsum = sb("rsum", [P, H])
        cw = sb("cw", [P, CI, TAPS])
        wx = sb("wx", [P, CI, 2 * DS])
        wlow = sb("wlow", [2 * DS, 2, DI])
        bdt = sb("bdt", [P, CI])
        dpar = sb("dpar", [P, CI])
        sc = sb("sc", [P, 3])

        sflat = scores2[:, :, :].rearrange("p a n -> p (a n)")
        at = [2 * 2 * DK * TW]

        def view(base, lo, n):
            return base[:, lo:lo + n]

        def place(n):
            v = view(sflat, at[0], n)
            at[0] += n
            return v

        half = TW // 2
        ctx_sb = [place(TC * D).rearrange("p (c d) -> p c d", c=TC) for _ in range(2)]
        ctxT_hi, ctxT_lo = [[ctx_split[:, j, i] for i in range(2)] for j in range(2)]
        rest_at = at[0]
        rest = [place(TW) for _ in range(2)]
        part1, part2, part3 = [[place(half).bitcast(BF16) for _ in range(G)] for _ in range(3)]
        vfull = [place(H * VT) for _ in range(2)]
        vtile = [v.rearrange("p (h n) -> p h n", h=H)[:, :, 0:TC * VW].rearrange("p h (c w) -> p h c w", c=TC)
                 for v in vfull]
        wkv = probs[:, :, :].rearrange("p a n -> p (a n)")[:, 0:DK * (G * P + D)]
        wk = wkv[:, 0:DK * G * P].rearrange("p (k n) -> p k n", k=DK)
        wv = wkv[:, DK * G * P:].rearrange("p (k n) -> p k n", k=DK)
        wkv_hi, wkv_lo = [wkv_split[:, j] for j in range(2)]
        wk_hi, wk_lo = [w[:, 0:DK * G * P].rearrange("p (k n) -> p k n", k=DK) for w in (wkv_hi, wkv_lo)]
        wv_hi, wv_lo = [w[:, DK * G * P:].rearrange("p (k n) -> p k n", k=DK) for w in (wkv_hi, wkv_lo)]
        wq = pt[:, :, :].rearrange("p a n -> p (a n)")[:, 0:DK * G * P].rearrange("p (k n) -> p k n", k=DK)
        bv_bc = place(D)
        qrest = pt[:, :, :].rearrange("p a n -> p (a n)")[:, DK * G * P:DK * G * P + G * P]
        qf = place(G * P)
        qstage = place(G * (NPART + 1) * P).bitcast(BF16).rearrange("p (s g b q) -> p s g b q", s=NPART + 1, g=G, b=2)
        assert at[0] <= 2 * NT * TW, at

        kflat = kring[:, :].bitcast(FP32)
        w_in = view(kflat, 0, DK * 2 * DI).rearrange("p (k n) -> p k n", k=DK)
        w_out = view(kflat, DK * 2 * DI, CI * D).rearrange("p (k n) -> p k n", k=CI)
        vt = [0]

        def room(n):
            v = view(sflat, NT * TW + vt[0], n)
            vt[0] += n
            return v

        x1, x1n, x2, x2n, fin, x0b = room(D), room(D), room(D), room(D), room(D), room(D)
        x1nT = room(D).rearrange("p (k n) -> p k n", k=DK)
        x2nT = room(D).rearrange("p (k n) -> p k n", k=DK)
        attT = room(D).rearrange("p (k n) -> p k n", k=DK)
        xpad = room(CI * (P + TAPS)).rearrange("p (c n) -> p c n", c=CI)
        mark = vt[0]
        c4 = lambda: room(CI * P).rearrange("p (c n) -> p c n", c=CI)
        z_sb, conv, conv2, u, e1, e2, dt, sp, absd, keep, hs, y, bp, ub, sz = [c4() for _ in range(15)]
        xp = room(P)
        FT = F1 // P
        FB = FT // 2
        assert vt[0] <= NT * TW
        vt[0] = mark
        f32h = [room(FT * P) for _ in range(2)]
        frest = room(FT * P)
        hp = [[room(FT * P // 2).bitcast(BF16) for _ in range(3)] for _ in range(3)]
        assert vt[0] <= NT * TW
        K0R, K1R, K2R = 2 * D // P, F1 // P, F1 // P
        w8n = (K0R * F1 + K1R * F1 + K2R * D) // 4
        w8 = view(sflat, 0, w8n).bitcast(U8)
        K0 = D // P
        wbn = (K0 * F1 + K1R * F1 + K2R * D) // 2
        W8T = -(-w8n // TW)
        wb = view(sflat, W8T * TW, wbn).bitcast(BF16)
        assert W8T * TW + wbn <= NT * TW
        o1, o2 = K0R * F1, (K0R + K1R) * F1
        b1, b2 = K0 * F1, (K0 + K1R) * F1
        w0x = view(sflat, W8T * TW + wbn, K0 * F1).bitcast(BF16)
        assert W8T * TW + wbn + K0 * F1 <= NT * TW
        w0b = wb[:, 0:b1].rearrange("p (k n) -> p k n", k=K0)
        w1b = wb[:, b1:b2].rearrange("p (k n) -> p k n", k=K1R)
        w2b = wb[:, b2:b2 + K2R * D].rearrange("p (k n) -> p k n", k=K2R)

        psA = [pb(f"psA{i}", [P, 2, 512]) for i in range(2)]
        psT = pb("psT", [P, 2, 512])
        psTf, psAf = [v[:, :, :].rearrange("p a n -> p (a n)") for v in (psT, psA[1])]
        psO = pb("psO", [P, 512])
        psM = pb("psM", [P, 512])
        psH = (psO, psM)
        assert NT % 4 == 2 and KRING * 2 == NT

        s_bq = sem("query_bias_and_pos_in")
        s_ld = sem("last_stage_parameters_in")
        s_x0 = sem("x_in")
        s_bkv = sem("key_value_biases_in")
        s_ctx = [sem(f"ctx_in{i}") for i in range(2)]
        s_wload = sem("key_value_weights_in")
        s_wq = sem("query_weights_in")
        s_wh = sem("weights_high_ready")
        s_ws = sem("weights_split")
        s_id = sem("identity_ready")
        s_one = sem("ones_ready")
        s_ln = sem("ln_chain")
        s_sq = sem("ln_sqrt")
        s_sv = sem("ln_var_ready")
        s_xn = sem("xn_ready")
        s_xt = sem("xn_transposed")
        s_xc = sem("xnT_ready")
        s_qm = sem("q_projected")
        s_qt = sem("q_taken")
        s_qp = sem("q_parts_ready")
        s_qw = sem("q_rows_written")
        s_qs = sem("q_stack_loaded")
        s_tp = sem("ctx_transposed")
        s_ch = sem("ctxT_high_ready")
        s_ct = sem("ctxT_ready")
        s_kp = sem("key_projected")
        s_k1 = sem("key_part1_ready")
        s_r = sem("key_rest_ready")
        s_k2 = sem("key_part2_ready")
        s_k3 = sem("key_part3_ready")
        s_kw = [sem(f"key_rows_written{g}") for g in range(G)]
        s_vm = sem("values_projected")
        s_v = sem("values_ready")
        s_kin = [sem(f"key_tile_in{i}") for i in range(KRING)]
        s_mm = sem("scores_in_psum")
        s_cp = sem("scores_in_sbuf")
        s_exp = sem("exp_ready")
        s_msf = sem("masked_first_chunks")
        s_msk = sem("masked_ready")
        s_t1 = sem("probs_transposed")
        s_e0 = sem("pt_ready")
        s_pv = sem("weighted_sum_added")
        s_vw = [sem(f"values_written{i}") for i in range(2)]
        s_vin = [sem(f"values_in{i}") for i in range(2)]
        s_max = sem("candidates_ready")
        s_lk = sem("threshold_chain")
        s_thr = sem("threshold_ready")
        s_fl = sem("flag_ready")
        s_fs = sem("flag_summed")
        s_fi = sem("flag_int_ready")
        s_gen = sem("general_path_chain")
        s_oev = sem("head_output_taken")
        s_w3 = sem("state_weights_in")
        s_w8 = sem("ffn_bytes_in")
        s_wx = sem("ffn_layer0_bytes_converted")
        s_wb = sem("ffn_weights_ready")
        s_dv = sem("tail_vector_chain")
        T = {n: sem(n) for n in (
            "sums_done", "att_ready", "att_turned", "attT_ready", "wo_done", "var1", "std1", "x1n_ready",
            "x1n_turned", "x1nT_ready", "xc_done", "z_done", "xpad_ready", "conv_ready", "u_exp", "z_exp",
            "u_ready", "low_rank_done", "xp_ready", "dt_done",
            "bp_done", "abs_ready", "dt_exp", "dt_ln", "y_ready", "mix_done", "var2", "std2", "x2n_ready",
            "x2n_turned", "x2nT_ready", "in_parts", "ffn0_done", "h0_parts", "ffn1_done", "h1_parts", "ffn2_done",
            "z_taken", "output")}
        s_out = sem("output_written")

        block = ctx.enter_context(nc.Block())
        KW = 16 * NPART
        SMALL = 11

        def flat(v):
            return v.rearrange("p c n -> p (c n)")

        def slot(par, t):
            return (t + 2 * par) % 4

        def turned(hB, t):
            return psAf if isinstance(hB, int) and hB >= H - 2 and t % 2 else psTf

        def xc_bank(c):
            return psA[c // 2][:, c % 2, 0:P]

        def scalar_tail(act):
            def wait(n):
                act.wait_ge(T[n], 1)

            def f(dst, src, func, done, **kw):
                nc.scalar.activation(dst, src, func, **kw).then_inc(T[done], 1)

            wait("att_turned")
            f(flat(attT), psM[:, 0:D], ACT.Copy, "attT_ready")
            wait("var1")
            f(rstd[:, 0:1], mv[:, 1:2], ACT.Sqrt, "std1")
            wait("x1n_turned")
            f(flat(x1nT), psM[:, 0:D], ACT.Copy, "x1nT_ready")
            for c in range(CI):
                act.wait_ge(T["xc_done"], c + 1)
                f(xpad[:, c, TAPS:], xc_bank(c), ACT.Copy, "xpad_ready")
            for j in range(2):
                act.wait_ge(T["conv_ready"], 2 * (j + 1))
                f(flat(e1[:, 2 * j:2 * j + 2, :]), flat(conv[:, 2 * j:2 * j + 2, :]), ACT.Exp, "u_exp", scale=-1.0)
            wait("z_done")
            f(flat(z_sb), psT[:, 0, :], ACT.Copy, "z_taken")
            wait("z_taken")
            f(flat(e2), flat(z_sb), ACT.Exp, "z_exp", scale=-1.0)
            wait("abs_ready")
            f(flat(sp), flat(absd), ACT.Exp, "dt_exp", scale=-1.0)
            wait("dt_exp")
            f(flat(sp), flat(sp), ACT.Ln, "dt_ln", bias=ones[:, :])
            wait("var2")
            f(rstd[:, 0:1], mv[:, 1:2], ACT.Sqrt, "std2")
            wait("x2n_turned")
            f(flat(x2nT), psM[:, 0:D], ACT.Copy, "x2nT_ready")

        def add_column_tiles(heads):
            for h in heads:
                last = nc.tensor.matmul(psA[0][:, 0, h * VW:(h + 1) * VW], outT[:, h + 1, :], select[:, :],
                                        start=True, stop=True)
            return last

        def tensor_tail(pe):
            def turn_rows(src, ready, done):
                pe.wait_ge(*ready)
                for k in range(DK):
                    last = nc.tensor.transpose(psM[:, k * P:(k + 1) * P], src[:, k * P:(k + 1) * P], ident[:, :])
                last.then_inc(T[done], 1)

            pe.wait_ge(s_oev, H + 2)
            add_column_tiles(range(H - 1, H)).then_inc(T["sums_done"], 1)
            turn_rows(att, (T["att_ready"], 1), "att_turned")
            pe.wait_ge(T["attT_ready"], 1)
            pe.wait_ge(s_ld, 16 * SMALL)
            for k in range(DK):
                last = nc.tensor.matmul(psO[:, 0:D], attT[:, k, :], wo[:, k, :], start=(k == 0), stop=(k == DK - 1))
            last.then_inc(T["wo_done"], 1)
            turn_rows(x1n, (T["x1n_ready"], 1), "x1n_turned")
            pe.wait_ge(T["x1nT_ready"], 1)
            pe.wait_ge(s_w3, 32)
            for c in range(2 * CI):
                dst = xc_bank(c) if c < CI else psT[:, 0, (c - CI) * P:(c - CI + 1) * P]
                for k in range(DK):
                    last = nc.tensor.matmul(dst, w_in[:, k, c * P:(c + 1) * P], x1nT[:, k, :],
                                            start=(k == 0), stop=(k == DK - 1))
                if c < CI:
                    last.then_inc(T["xc_done"], 1)
            last.then_inc(T["z_done"], 1)
            for c in range(CI):
                if c % 2 == 0:
                    pe.wait_ge(T["u_ready"], c // 2 + 1)
                last = nc.tensor.matmul(psM[0:2 * DS, 0:P], wx[:, c, :], u[:, c, :], start=(c == 0), stop=(c == CI - 1))
            last.then_inc(T["low_rank_done"], 1)
            pe.wait_ge(T["xp_ready"], 1)
            pe.wait_ge(T["z_taken"], 1)
            for j, done in enumerate(("dt_done", "bp_done")):
                for c in range(CI):
                    cols = slice(c * P, (c + 1) * P)
                    last = nc.tensor.matmul(psT[:, 1 - j, cols], wlow[:, j, cols], xp[0:2 * DS, :], start=True,
                                            stop=True)
                last.then_inc(T[done], 1)
            for c in range(CI):
                if c % 2 == 0:
                    pe.wait_ge(T["y_ready"], c // 2 + 1)
                last = nc.tensor.matmul(psO[:, 0:D], y[:, c, :], w_out[:, c, :], start=(c == 0), stop=(c == CI - 1))
            last.then_inc(T["mix_done"], 1)
            turn_rows(x2n, (T["x2n_ready"], 1), "x2n_turned")

            def products(w, parts, ps, fts, ks, rows):
                for ft in fts:
                    for k in ks:
                        for i in range(3):
                            last = nc.tensor.matmul(ps[:, ft // FB, (ft % FB) * P:(ft % FB + 1) * P],
                                                    w[:, k, ft * P:(ft + 1) * P], parts[i][:, k * P:(k + 1) * P],
                                                    start=(ft % FB == 0 and k == 0 and i == 0),
                                                    stop=(ft % FB == FB - 1 and k == rows - 1 and i == 2))
                return last

            pe.wait_ge(s_wb, 3)
            pe.wait_ge(T["in_parts"], 1)
            for b in range(2):
                products(w0b, hp[0], psA[0], range(b * FB, (b + 1) * FB), range(K0), K0).then_inc(T["ffn0_done"], 1)
            pe.wait_ge(T["h0_parts"], 1)
            products(w1b, hp[1], psA[1], range(FT), range(FB), K1R)
            pe.wait_ge(T["h0_parts"], 2)
            for b in range(2):
                products(w1b, hp[1], psA[1], range(b * FB, (b + 1) * FB), range(FB, FT), K1R)\
                    .then_inc(T["ffn1_done"], 1)
            for k in range(K2R):
                if k % FB == 0:
                    pe.wait_ge(T["h1_parts"], k // FB + 1)
                for i in range(3):
                    last = nc.tensor.matmul(psO[:, 0:D], hp[2][i][:, k * P:(k + 1) * P], w2b[:, k, :],
                                            start=(k == 0 and i == 0), stop=(k == K2R - 1 and i == 2))
            last.then_inc(T["ffn2_done"], 1)

        def vector_tail(dve):
            cnt = [0]

            def link(ins):
                cnt[0] += 1
                ins.then_inc(s_dv, 1)
                dve.wait_ge(s_dv, cnt[0])

            def each(make, chunks=range(CI)):
                for c in chunks:
                    cnt[0] += 1
                    make(c).then_inc(s_dv, 1)
                dve.wait_ge(s_dv, cnt[0])

            V = nc.vector

            def norm(src, dst, var, std, ready):
                link(V.bn_stats(stats[:, :], src))
                link(V.bn_aggr(mv[:, :], stats[:, :]))
                V.tensor_scalar(mv[:, 1:2], mv[:, 1:2], EPS, None, ALU.add).then_inc(T[var], 1)
                dve.wait_ge(T[std], 1)
                link(V.reciprocal(rstd[:, 1:2], rstd[:, 0:1]))
                V.tensor_scalar(dst, src, mv[:, 0:1], rstd[:, 1:2], ALU.subtract, ALU.mult).then_inc(T[ready], 1)

            link(V.memset(flat(xpad), 0.0))
            dve.wait_ge(s_ld, 16 * SMALL)
            link(V.tensor_tensor(out=x0b, in0=x0[:, :], in1=bo_bc[:, :], op=ALU.add))
            link(V.tensor_scalar(sc[:, 0:1], sc[:, 0:1], 4.0, None, ALU.mult))
            link(V.tensor_scalar(sc[:, 1:2], sc[:, 1:2], 2.0, None, ALU.mult))
            dve.wait_ge(T["sums_done"], 1)
            sums = psA[0][:, 0, 0:H * VW].rearrange("p (h w) -> p h w", w=VW)
            link(V.reciprocal(rsum[:, :], sums[:, :, DH:VW].rearrange("p h w -> p (h w)")))
            V.tensor_tensor(out=att[:, :].rearrange("p (h d) -> p h d", h=H), in0=sums[:, :, 0:DH],
                            in1=rsum[:, :].rearrange("p (h w) -> p h w", w=1).broadcast_to([P, H, DH]),
                            op=ALU.mult).then_inc(T["att_ready"], 1)
            dve.wait_ge(T["wo_done"], 1)
            link(V.tensor_tensor(out=x1, in0=psO[:, 0:D], in1=x0b, op=ALU.add))
            norm(x1, x1n, "var1", "std1", "x1n_ready")
            for pair in (range(0, 2), range(2, 4)):
                dve.wait_ge(T["xpad_ready"], pair[-1] + 1)
                each(lambda c: V.tensor_scalar(conv2[:, c, :], xpad[:, c, 1:1 + P], cw[:, c, 0:1], None, ALU.mult),
                     pair)
                for j in range(1, TAPS - 1):
                    src, dst = (conv2, conv) if j % 2 else (conv, conv2)
                    each(lambda c: V.scalar_tensor_tensor(out=dst[:, c, :], in0=xpad[:, c, 1 + j:1 + j + P],
                                                          scalar=cw[:, c, j:j + 1], in1=src[:, c, :], op0=ALU.mult,
                                                          op1=ALU.add), pair)
                for c in pair:
                    V.scalar_tensor_tensor(out=conv[:, c, :], in0=xpad[:, c, TAPS:TAPS + P],
                                           scalar=cw[:, c, TAPS - 1:TAPS], in1=conv2[:, c, :], op0=ALU.mult,
                                           op1=ALU.add).then_inc(T["conv_ready"], 1)
            for j in range(2):
                e1j, cj, uj = [flat(v[:, 2 * j:2 * j + 2, :]) for v in (e1, conv, u)]
                dve.wait_ge(T["u_exp"], j + 1)
                link(V.tensor_scalar(e1j, e1j, 1.0, None, ALU.add))
                link(V.reciprocal(e1j, e1j))
                V.tensor_tensor(out=uj, in0=cj, in1=e1j, op=ALU.mult).then_inc(T["u_ready"], 1)
            dve.wait_ge(T["low_rank_done"], 1)
            V.tensor_copy(xp[0:2 * DS, :], psM[0:2 * DS, 0:P]).then_inc(T["xp_ready"], 1)
            dve.wait_ge(T["z_exp"], 1)
            link(V.tensor_scalar(flat(e2), flat(e2), 1.0, None, ALU.add))
            half = [flat(e2[:, 2 * j:2 * j + 2, :]) for j in range(2)]
            link(V.reciprocal(half[0], half[0]))
            dve.wait_ge(T["dt_done"], 1)
            each(lambda c: V.tensor_scalar(dt[:, c, :], psT[:, 1, c * P:(c + 1) * P], bdt[:, c:c + 1], None, ALU.add))
            link(V.tensor_scalar(flat(e1), flat(dt), -1.0, None, ALU.mult))
            V.tensor_tensor(out=flat(absd), in0=flat(dt), in1=flat(e1), op=ALU.max).then_inc(T["abs_ready"], 1)
            dve.wait_ge(T["bp_done"], 1)
            dve.wait_ge(T["u_ready"], 2)
            link(V.tensor_tensor(out=flat(ub), in0=psT[:, 0, :], in1=flat(u), op=ALU.mult))
            link(V.reciprocal(half[1], half[1]))
            link(V.tensor_tensor(out=flat(sz), in0=flat(z_sb), in1=flat(e2), op=ALU.mult))
            dve.wait_ge(T["dt_ln"], 1)
            link(V.scalar_tensor_tensor(out=flat(dt), in0=flat(dt), scalar=0.0, in1=flat(sp), op0=ALU.max,
                                        op1=ALU.add))
            link(V.tensor_scalar(flat(dt), flat(dt), 1e-4, 1.0, ALU.max, ALU.min))
            link(V.tensor_scalar(flat(keep), flat(dt), -1.0, 1.0, ALU.mult, ALU.add))
            for pair in (range(0, 2), range(2, 4)):
                each(lambda c: V.tensor_tensor_scan(hs[:, c, :], keep[:, c, :], ub[:, c, :], 0.0, ALU.mult, ALU.add),
                     pair)
                each(lambda c: V.scalar_tensor_tensor(out=y[:, c, :], in0=u[:, c, :], scalar=dpar[:, c:c + 1],
                                                      in1=hs[:, c, :], op0=ALU.mult, op1=ALU.add), pair)
                yj, szj = [flat(v[:, pair[0]:pair[0] + 2, :]) for v in (y, sz)]
                V.tensor_tensor(out=yj, in0=yj, in1=szj, op=ALU.mult).then_inc(T["y_ready"], 1)
            dve.wait_ge(T["mix_done"], 1)
            link(V.tensor_tensor(out=x2, in0=psO[:, 0:D], in1=x1, op=ALU.add))
            norm(x2, x2n, "var2", "std2", "x2n_ready")

            def parts(src, cols, dst, done):
                p1, p2, p3 = [d[:, cols] for d in dst]
                r = frest[:, cols]
                link(V.tensor_copy(p1, src))
                link(V.tensor_tensor(out=r, in0=src, in1=p1, op=ALU.subtract))
                link(V.tensor_copy(p2, r))
                V.tensor_tensor(out=p3, in0=r, in1=p2, op=ALU.subtract).then_inc(T[done], 1)

            dve.wait_ge(T["x2nT_ready"], 1)
            parts(flat(x2nT), slice(0, D), hp[0], "in_parts")
            for i, (ready, done) in enumerate((("ffn0_done", "h0_parts"), ("ffn1_done", "h1_parts"))):
                for b in range(2):
                    cols = slice(b * FB * P, (b + 1) * FB * P)
                    dve.wait_ge(T[ready], b + 1)
                    link(V.tensor_scalar(f32h[i][:, cols], psA[i][:, b, :], sc[:, i:i + 1], 0.0, ALU.mult, ALU.max))
                    parts(f32h[i][:, cols], cols, hp[i + 1], done)
            dve.wait_ge(T["ffn2_done"], 1)
            V.scalar_tensor_tensor(out=fin, in0=psO[:, 0:D], scalar=sc[:, 2:3], in1=x2, op0=ALU.mult,
                                   op1=ALU.add).then_inc(T["output"], 1)

        @block.sync
        def _(sp):
            def load_ctx(t, i):
                src = a["ctx_1024"][0][bass.ds(t * TW, TW), :] if not isinstance(t, int) \
                    else a["ctx_1024"][0][t * TW:(t + 1) * TW, :]
                sp.dma_start(ctx_sb[i], src.rearrange("(c p) d -> p c d", p=P)).then_inc(s_ctx[i], 16)

            def weights(dst, name, done):
                sp.dma_start(dst, a[name].rearrange("(k p) n -> p k n", p=P)).then_inc(done, 16)

            load_ctx(0, 0)
            weights(wk, "L0_xattn_Wk", s_wload)
            weights(wv, "L0_xattn_Wv", s_wload)
            sp.dma_start(x0[:, :], a["x"][0]).then_inc(s_x0, 16)
            load_ctx(1, 1)
            weights(wq, "L0_xattn_Wq", s_wq)

            def key_writes(t):
                for g in range(G):
                    u = G * t + g
                    cols = bass.ds(t * TW, TW)
                    rows = slice(g * P, (g + 1) * P)
                    sp.wait_ge(s_k1, u + 1)
                    sp.dma_start(key_parts[rows, 0, cols], part1[g]).then_inc(s_kw[g], 16)
                    sp.wait_ge(s_k2, u + 1)
                    sp.dma_start(key_parts[rows, 1, cols], part2[g]).then_inc(s_kw[g], 16)
                    sp.wait_ge(s_k3, u + 1)
                    sp.dma_start(key_parts[rows, 2, cols], part3[g]).then_inc(s_kw[g], 16)

            def value_writes(t, i):
                sp.wait_ge(s_v, TC * (t + 1))
                sp.dma_start(value_rows[:, :, bass.ds(t * VT, VT)].rearrange("h p n -> p h n"),
                             vfull[i].rearrange("p (h n) -> p h n", h=H)).then_inc(s_vw[i], 16)

            for t in range(2):
                sp.wait_ge(s_tp, 2 * (t + 1))
                load_ctx(t + 2, t)
                key_writes(t)
                value_writes(t, t)
            sp.wait_ge(s_qp, 5)
            sp.wait_ge(s_one, 5)
            for n in range(NPART):
                sp.dma_start(qry_parts[:, :, n, :, :], qstage[:, n]).then_inc(s_qw, 16)
            sp.dma_start(qry_fourth, qstage[:, NPART]).then_inc(s_qw, 16)

            with sp.Fori(1, NT // 2 - 2) as i:
                for j in range(2):
                    sp.wait_ge(s_tp, 2 * (2 * i + j + 1))
                    load_ctx(2 * i + j + 2, j)
                    key_writes(2 * i + j)
                    value_writes(2 * i + j, j)
            sp.wait_ge(s_qw, 16 * (NPART + 1))
            sp.dma_start(qstack[0:RP, :, :, :], qry_rows.rearrange("(h p) b q -> p h b q", p=RP)).then_inc(s_qs, 16)
            sp.dma_start(qstack[RP:P, :, :, :], qry_again.rearrange("(h p) b q -> p h b q", p=R)).then_inc(s_qs, 16)

            def stream(h, t):
                cols = slice(t * TW, (t + 1) * TW)
                slot = slice((t % KRING) * TW, (t % KRING + 1) * TW)
                sp.dma_start(kring[0:RP, slot], key_rows[bass.ds(h * RP, RP), cols]).then_inc(s_kin[t % KRING], 16)
                sp.dma_start(kring[RP:P, slot], key_parts[bass.ds(h * R, R), 0, cols]).then_inc(s_kin[t % KRING], 16)

            for t in range(NT - 4, NT):
                if t + 2 < NT:
                    sp.wait_ge(s_tp, 2 * (t + 1))
                    load_ctx(t + 2, t % 2)
                key_writes(t)
                value_writes(t, t % 2)
                if t == NT - 4:
                    sp.wait_ge(s_kw[0], KW * KRING)
                if t < NT - 1:
                    for n in range(3 * (t - NT + 4), min(3 * (t - NT + 5), KRING)):
                        stream(0, n)
            sp.wait_ge(s_kw[0], KW * NT)
            for t in range(KRING, NT):
                sp.wait_ge(s_mm, t - KRING + 1)
                stream(0, t)
            for g in range(1, G):
                sp.wait_ge(s_kw[g], KW * NT)
            with sp.Fori(1, H) as h:
                for t in range(NT):
                    sp.wait_ge(s_mm, h * NT + (t - KRING + 1))
                    stream(h, t)
            def bcast(dst, src, n):
                sp.dma_start(dst, src.rearrange("(o n) -> o n", o=1).broadcast_to([P, n])).then_inc(s_ld, 16)

            def cols(dst, src):
                sp.dma_start(dst, src.rearrange("(g p) -> p g", p=P), allow_slow_non_contiguous=True)\
                    .then_inc(s_ld, 16)

            bcast(bo_bc[:, :], a["L0_xattn_bo"], D)
            sp.dma_start(wo[:, :, :], a["L0_xattn_Wo"].rearrange("(k p) n -> p k n", p=P)).then_inc(s_ld, 16)
            sp.dma_start(cw[:, :, :], a["L0_attn_conv_w"].rearrange("(c p) o k -> p c (o k)", p=P)).then_inc(s_ld, 16)
            sp.dma_start(wx[:, :, :], a["L0_attn_W_x"].rearrange("(c p) n -> p c n", p=P)).then_inc(s_ld, 16)
            sp.wait_ge(s_one, 5)
            sp.dma_start(wlow[0:DS, 0, :], a["L0_attn_W_dt"]).then_inc(s_ld, 16)
            sp.dma_start(wlow[DS:2 * DS, 1, :], a["L0_attn_W_Bp"]).then_inc(s_ld, 16)
            cols(bdt[:, :], a["L0_attn_b_dt"])
            cols(dpar[:, :], a["L0_attn_D_param"])
            for i in range(3):
                bcast(sc[:, i:i + 1], a[f"L0_ffn_s{i}"], 1)
            sp.wait_ge(s_mm, H * NT)
            sp.dma_start(w_in, a["L0_attn_W_in"].rearrange("(k p) n -> p k n", p=P)).then_inc(s_w3, 16)
            sp.dma_start(w_out, a["L0_attn_W_out"].rearrange("(k p) n -> p k n", p=P)).then_inc(s_w3, 16)
            sp.wait_ge(s_msk, (H - 2) * NT + W8T)
            for k, lo, rows, n in (("L0_ffn_k0", 0, K0R, F1), ("L0_ffn_k1", o1, K1R, F1), ("L0_ffn_k2", o2, K2R, D)):
                sp.dma_start(w8[:, lo:lo + rows * n].rearrange("p (k n) -> p k n", k=rows),
                             a[k].rearrange("(k p) n -> p k n", p=P)).then_inc(s_w8, 16)
            sp.wait_ge(T["output"], 1)
            sp.dma_start(out[0], fin).then_inc(s_out, 16)
            sp.wait_ge(s_out, 16)

        @block.gpsimd
        def _(pool):
            nc.gpsimd.memset(ident[:, :], 0.0).then_inc(s_id, 1)
            nc.gpsimd.memset(ones[:, :], 1.0).then_inc(s_one, 1)
            pool.wait_ge(s_id, 1)
            nc.gpsimd.affine_select(out=ident[:, :], in_=ident[:, :], compare_op=ALU.not_equal, fill=1.0, base=0,
                                    pattern=[[-1, P]], channel_multiplier=1).then_inc(s_id, 1)
            for i in range(2):
                nc.gpsimd.memset(vfull[i], 1.0).then_inc(s_one, 1)
            nc.gpsimd.memset(wlow[:, :, :], 0.0).then_inc(s_one, 1)
            nc.gpsimd.memset(qstage[:, NPART, :, 1, :], 0.0).then_inc(s_one, 1)

            def third_part(t, g):
                pool.wait_ge(s_k2, G * t + g + 1)
                if not (isinstance(t, int) and t == 0):
                    pool.wait_ge(s_kw[g], KW * t)
                nc.gpsimd.tensor_tensor(out=part3[g], in0=rest[g % 2], in1=part2[g],
                                        op=ALU.subtract).then_inc(s_k3, 1)

            for g in range(G):
                third_part(0, g)
            with pool.Fori(1, NT) as t:
                for g in range(G):
                    third_part(t, g)
            for i in range(2):
                pool.wait_ge(s_vw[i], 16 * NT // 2)
            pool.wait_ge(s_mm, NT)
            for i in range(2):
                pool.dma_start(vhead[:, i, :, :].rearrange("p t n -> p (t n)"), value_rows[i]).then_inc(s_vin[i], 16)
            with pool.Fori(0, (H - 2) // 2) as i:
                for j in range(2):
                    pool.wait_ge(s_pv, (2 * i + j + 1) * NT + 2)
                    pool.dma_start(vhead[:, j, :, :].rearrange("p t n -> p (t n)"),
                                   value_rows[bass.ds(2 * i + j + 2, 1)].rearrange("o p n -> (o p) n"))\
                        .then_inc(s_vin[j], 16)
            pool.wait_ge(s_w8, 48)
            pool.wait_ge(s_msk, (H - 1) * NT)
            for j in range(2):
                nc.gpsimd.tensor_scalar(w0x[:, j * b1:(j + 1) * b1], w8[:, j * b1:(j + 1) * b1], 1.0, 0.0, ALU.mult,
                                        ALU.add).then_inc(s_wx, 1)
            pool.wait_ge(s_wx, 2)
            nc.gpsimd.tensor_tensor(out=wb[:, 0:b1], in0=w0x[:, 0:b1], in1=w0x[:, b1:2 * b1],
                                    op=ALU.subtract).then_inc(s_wb, 1)
            for dst, lo, n in ((b1, o1, o2 - o1), (b2, o2, K2R * D)):
                nc.gpsimd.tensor_scalar(wb[:, dst:dst + n], w8[:, lo:lo + n], 2.0, -1.0, ALU.mult,
                                        ALU.add).then_inc(s_wb, 1)

        @block.scalar
        def _(act):
            def bcast(dst, src, n, done):
                act.dma_start(dst, src.rearrange("(o n) -> o n", o=1).broadcast_to([P, n])).then_inc(done, 16)

            def cols(dst, src, done):
                act.dma_start(dst, src.rearrange("(g p) -> p g", p=P), allow_slow_non_contiguous=True)\
                    .then_inc(done, 16)

            cols(bk[:, :], a["L0_xattn_bk"], s_bkv)
            bcast(bv_bc, a["L0_xattn_bv"], D, s_bkv)
            cols(bq[:, :], a["L0_xattn_bq"], s_bq)
            bcast(pos[:, :], a["L0_xattn_pos_bias"].rearrange("a h b c -> (a h b c)"), H, s_bq)

            def take_ctxT(t, i, k):
                act.wait_ge(s_tp, 2 * t + k + 1)
                if k == 0:
                    act.wait_ge(s_vm, TC * t)
                nc.scalar.activation(ctxT_hi[i][:, k, :], psTf[:, 0:TW], ACT.Copy).then_inc(s_ch, 1)

            def take_part1(t, g):
                u = G * t + g
                act.wait_ge(s_kp, u + 1)
                if not (isinstance(t, int) and t == 0):
                    act.wait_ge(s_kw[g], KW * t)
                nc.scalar.activation(part1[g].rearrange("p (a n) -> p a n", a=2), psA[g % 2][:, :, 0:HW],
                                     ACT.Identity, bias=bk[:, g:g + 1]).then_inc(s_k1, 1)

            def take_part2(t, g):
                act.wait_ge(s_r, G * t + g + 3)
                nc.scalar.activation(part2[g], rest[g % 2], ACT.Copy).then_inc(s_k2, 1)

            def key_tile(t, i, more):
                if more:
                    take_ctxT(t + 1, 1 - i, 0)
                for g in range(G):
                    if more and g == TURN_G:
                        take_ctxT(t + 1, 1 - i, 1)
                    take_part1(t, g)
                    if isinstance(t, int) and t == 1 and g == 0:
                        act.wait_ge(s_xt, 1)
                        nc.scalar.activation(xnT[:, :, :], psM[:, 0:D].rearrange("p (k n) -> p k n", k=DK),
                                             ACT.Copy).then_inc(s_xc, 1)
                    if g > 0:
                        take_part2(t, g - 1)
                take_part2(t, G - 1)

            take_ctxT(0, 0, 0)
            act.wait_ge(s_wload, 32)
            nc.scalar.activation(wkv_hi, wkv, ACT.Copy).then_inc(s_wh, 1)
            take_ctxT(0, 0, 1)
            act.wait_ge(s_bkv, 32)
            act.wait_ge(s_sv, 1)
            nc.scalar.activation(rstd[:, 0:1], mv[:, 1:2], ACT.Sqrt).then_inc(s_sq, 1)
            key_tile(0, 0, True)
            key_tile(1, 1, True)
            with act.Fori(1, NT // 2 - 1) as i:
                for j in range(2):
                    key_tile(2 * i + j, j, True)
            key_tile(NT - 2, 0, True)
            key_tile(NT - 1, 1, False)

            def copy_scores(hA, par, t):
                n = hA * NT + t
                act.wait_ge(s_mm, n + 1)
                if not (isinstance(hA, int) and hA < 2):
                    act.wait_ge(s_msk, n - 2 * NT + 1)
                elif t == 0 and par == 0:
                    act.wait_ge(s_vm, TC * (NT + 1))
                elif par == 0 and (t + 1) * TW > rest_at and t * TW <= rest_at:
                    act.wait_ge(s_k3, G * NT)
                elif t == 0:
                    for g in range(G):
                        act.wait_ge(s_kw[g], KW * NT)
                    for i in range(2):
                        act.wait_ge(s_vw[i], 8 * NT)
                nc.scalar.activation(scores2[:, par, t * TW:(t + 1) * TW].rearrange("p (a n) -> p a n", a=2),
                                     psA[t % 2][:, :, 0:HW], ACT.Copy).then_inc(s_cp, 1)

            def exps(hB, par, t):
                m = hB * NT + t
                if t == 0:
                    act.wait_ge(s_thr, hB + 1)
                act.wait_ge(s_t1, m + 1)
                nc.scalar.activation(probs[:, slot(par, t), :], scores2[:, par, t * TW:(t + 1) * TW], ACT.Exp,
                                     bias=nbias[:, par:par + 1]).then_inc(s_exp, 1)

            def take_pt(hB, t):
                m = hB * NT + t
                act.wait_ge(s_pv, m + 1)
                act.wait_ge(s_t1, m + 5)
                nc.scalar.activation(pt[:, t % 2, :], turned(hB, t)[:, 0:TW], ACT.Copy).then_inc(s_e0, 1)

            def head(hB, hA, par, more=True):
                for t in range(NT):
                    if hB is not None and t + 2 < NT:
                        exps(hB, par, t + 2)
                    elif hB is not None and more:
                        exps(hB + 1, 1 - par, t + 2 - NT)
                    if hA is not None:
                        copy_scores(hA, par, t)
                    if hB is not None:
                        take_pt(hB, t)

            for par in range(2):
                head(None, par, par)
            for t in range(2):
                exps(0, 0, t)
            with act.Fori(0, H // 2 - 1) as i:
                for par in range(2):
                    head(2 * i + par, 2 * i + par + 2, par)
            head(H - 2, None, 0)
            head(H - 1, None, 1, more=False)
            scalar_tail(act)

        @block.tensor
        def _(pe):
            pe.sem_inc(s_vm, TC)
            pe.sem_inc(s_t1, 4)
            pe.sem_inc(s_pv, 2)
            pe.sem_inc(s_e0, 1)
            pe.sem_inc(s_oev, 1)
            pe.wait_ge(s_id, 2)

            def turn_queries():
                pe.wait_ge(s_xn, 1)
                pe.wait_ge(s_v, TC)
                for k in range(DK):
                    last = nc.tensor.transpose(psM[:, k * P:(k + 1) * P], xn[:, k * P:(k + 1) * P], ident[:, :])
                last.then_inc(s_xt, 1)

            def project_queries():
                pe.wait_ge(s_wq, 16)
                pe.wait_ge(s_v, TC + 2 * TURN_G)
                for g in range(G):
                    for k in range(DK):
                        last = nc.tensor.matmul(psO[:, g * P:(g + 1) * P], wq[:, k, g * P:(g + 1) * P], xnT[:, k, :],
                                                start=(k == 0), stop=(k == DK - 1))
                last.then_inc(s_qm, 1)

            def turn_ctx(t, i, k):
                if k == 0:
                    n = (t // 2 + 1) if isinstance(t, int) else None
                    pe.wait_ge(s_ctx[i], 16 * n if n is not None else 8 * (t - i) + 16)
                pe.wait_ge(s_ct, 2 * t + k)
                for c in range(TC):
                    last = nc.tensor.transpose(psTf[:, c * P:(c + 1) * P], ctx_sb[i][:, c, k * P:(k + 1) * P],
                                               ident[:, :])
                last.then_inc(s_tp, 1)

            def project_keys(t, i, g):
                if g == 0:
                    pe.wait_ge(s_ct, 2 * t + 2)
                pe.wait_ge(s_r, G * t + g + 1)
                for a_ in range(2):
                    for k in range(DK):
                        for n, (w, x) in enumerate(((wk_hi, ctxT_hi), (wk_hi, ctxT_lo), (wk_lo, ctxT_hi))):
                            last = nc.tensor.matmul(psA[g % 2][:, a_, 0:HW], w[:, k, g * P:(g + 1) * P],
                                                    x[i][:, k, a_ * HW:(a_ + 1) * HW],
                                                    start=(k == 0 and n == 0), stop=(k == DK - 1 and n == 2))
                last.then_inc(s_kp, 1)

            def project_values(t, i, chunks):
                for c in chunks:
                    if isinstance(t, int) and t == 1 and c == 1:
                        pe.wait_ge(s_xc, 1)
                    w = TC * t + c
                    bank = (psO, psM)[c % 2]
                    if c == 0 and not (isinstance(w, int) and w == 0):
                        pe.wait_ge(s_v, w)
                    elif c > 1:
                        pe.wait_ge(s_v, w - 1)
                    for k in range(DK):
                        for n, (x, w) in enumerate(((ctxT_hi, wv_hi), (ctxT_hi, wv_lo), (ctxT_lo, wv_hi))):
                            last = nc.tensor.matmul(bank[:, 0:D], x[i][:, k, c * P:(c + 1) * P], w[:, k, :],
                                                    start=(k == 0 and n == 0), stop=(k == DK - 1 and n == 2))
                    last.then_inc(s_vm, 1)

            def key_tile(t, i, more):
                if more:
                    turn_ctx(t + 1, 1 - i, 0)
                for g in range(G):
                    if more and g == TURN_G:
                        turn_ctx(t + 1, 1 - i, 1)
                    if isinstance(t, int) and t == 1 and g == TURN_G:
                        project_queries()
                    project_keys(t, i, g)
                    if isinstance(t, int) and t == 1 and g == 0:
                        turn_queries()
                    if isinstance(t, int) and t == 1 and g == TURN_G:
                        pe.wait_ge(s_qt, 1)
                    project_values(t, i, range(2 * g, min(2 * g + 2, TC)))

            turn_ctx(0, 0, 0)
            turn_ctx(0, 0, 1)
            pe.wait_ge(s_ws, 1)
            for t in range(2):
                key_tile(t, t, True)
            with pe.Fori(1, NT // 2 - 1) as i:
                for j in range(2):
                    key_tile(2 * i + j, j, True)
            key_tile(NT - 2, 0, True)
            key_tile(NT - 1, 1, False)

            def score_tile(hA, t):
                n = hA * NT + t
                pe.wait_ge(s_kin[t % KRING], 32 * (2 * hA + t // KRING + 1))
                if not (isinstance(hA, int) and n < 2):
                    pe.wait_ge(s_cp, n - 1)
                else:
                    pe.wait_ge(s_r, G * NT + n + 1)
                for a_ in range(2):
                    cols = kring[:, (t % KRING) * TW + a_ * HW:(t % KRING) * TW + (a_ + 1) * HW]
                    for b in range(2):
                        lhsT = qstack[:, hA, b, :] if isinstance(hA, int) else qstack[:, bass.ds(hA, 1), b, :]\
                            .rearrange("p o q -> p (o q)")
                        last = nc.tensor.matmul(psA[t % 2][:, a_, 0:HW], lhsT, cols, start=(b == 0), stop=(b == 1))
                last.then_inc(s_mm, 1)

            def turn(hB, par, t):
                m = hB * NT + t
                halves = isinstance(hB, int) and hB >= H - 2
                if halves:
                    pe.wait_ge(s_msf, m - (H - 2) * NT + 1)
                else:
                    pe.wait_ge(s_msk, m + 1)
                if halves and t == 1 and hB == H - 2:
                    pe.wait_ge(s_cp, H * NT)
                elif halves and m > (H - 2) * NT:
                    pe.wait_ge(s_e0, m)
                else:
                    pe.wait_ge(s_e0, m + 1)
                for c in range(TC):
                    if halves and c == C0:
                        pe.wait_ge(s_msk, m + 1)
                    cols = slice(c * P, (c + 1) * P)
                    last = nc.tensor.transpose(turned(hB, t)[:, cols], probs[:, slot(par, t), cols], ident[:, :])
                last.then_inc(s_t1, 1)

            def weigh(hB, par, t):
                m = hB * NT + t
                pe.wait_ge(s_e0, m + 2)
                if t == 0:
                    pe.wait_ge(s_oev, hB + 1)
                    pe.wait_ge(s_vin[par], 16 * (hB + 2 - par) // 2 if isinstance(hB, int) else 8 * (hB + 2 - par))
                for c in range(TC):
                    q = c % NQ
                    last = nc.tensor.matmul(psH[par][QUAD * q:QUAD * q + VW, 0:P],
                                            vhead[:, par, t, c * VW:(c + 1) * VW],
                                            pt[:, t % 2, c * P:(c + 1) * P], start=(t == 0 and c < NQ),
                                            stop=(t == NT - 1 and c >= TC - NQ))
                last.then_inc(s_pv, 1)

            def sum_flags(hT, par):
                pe.wait_ge(s_fl, hT + 1)
                nc.tensor.matmul(psH[par][0:1, 2 * P:2 * P + 1], flag[:, 0:1], ones[:, :], start=True, stop=True)\
                    .then_inc(s_fs, 1)

            def head(hB, hA, hT, par, more=True):
                for t in range(NT):
                    if hB is not None:
                        turn(hB, par, t)
                    if hA is not None and t + 1 < NT:
                        score_tile(hA, t + 1)
                    elif hA is not None and more:
                        score_tile(hA + 1, 0)
                    if hB is not None and t > 0:
                        weigh(hB, par, t - 1)
                    if hA is None and hT is None and t >= 4:
                        pe.wait_ge(s_oev, H + 1)
                        if t < 4 + H // 2:
                            add_column_tiles(range(2 * (t - 4), min(2 * (t - 3), H - 1)))
                    if hT is not None and t == (FLAG_T if hB is not None else NT - 1):
                        sum_flags(hT, 1 - par)
                if hB is not None:
                    weigh(hB, par, NT - 1)

            pe.wait_ge(s_qs, 32)
            score_tile(0, 0)
            head(None, 0, None, 0)
            pe.wait_ge(s_v, TC * NT)
            head(None, 1, 0, 1)
            with pe.Fori(0, H // 2 - 2) as i:
                for par in range(2):
                    head(2 * i + par, 2 * i + par + 2, 2 * i + par + 1, par)
            head(H - 4, H - 2, H - 3, 0)
            head(H - 3, H - 1, H - 2, 1, more=False)
            head(H - 2, None, H - 1, 0)
            head(H - 1, None, None, 1)
            tensor_tail(pe)

        @block.vector
        def _(dve):
            dve.sem_inc(s_r, 2)
            n_ln = [0]

            def link(ins):
                n_ln[0] += 1
                ins.then_inc(s_ln, 1)
                dve.wait_ge(s_ln, n_ln[0])

            def query_variance():
                dve.wait_ge(s_x0, 16)
                link(nc.vector.bn_stats(stats[:, :], x0[:, :]))
                link(nc.vector.bn_aggr(mv[:, :], stats[:, :]))
                nc.vector.tensor_scalar(mv[:, 1:2], mv[:, 1:2], EPS, None, ALU.add).then_inc(s_sv, 1)

            def make_select():
                dve.wait_ge(s_id, 2)
                link(nc.vector.tensor_tensor(out=select[:, :], in0=ident[:, 0:VW], in1=ident[:, QUAD:QUAD + VW],
                                             op=ALU.add))
                for q in range(2, NQ):
                    link(nc.vector.tensor_tensor(out=select[:, :], in0=select[:, :],
                                                 in1=ident[:, QUAD * q:QUAD * q + VW], op=ALU.add))

            def query_norm():
                dve.wait_ge(s_sq, 1)
                link(nc.vector.reciprocal(rstd[:, 1:2], rstd[:, 0:1]))
                nc.vector.tensor_scalar(xn[:, :], x0[:, :], mv[:, 0:1], rstd[:, 1:2], ALU.subtract,
                                        ALU.mult).then_inc(s_xn, 1)

            def take_queries():
                dve.wait_ge(s_bq, 32)
                dve.wait_ge(s_qm, 1)
                for g in range(G):
                    link(nc.vector.tensor_scalar(qf[:, g * P:(g + 1) * P], psO[:, g * P:(g + 1) * P], bq[:, g:g + 1],
                                                 1.0 / math.sqrt(R), ALU.add, ALU.mult))
                dve.sem_inc(s_qt, 1)

            def query_parts():
                V = nc.vector
                q1, q2, q3 = [qstage[:, s, :, b, :] for s, b in ((0, 0), (1, 1), (0, 1))]
                f, r = [v.rearrange("p (g q) -> p g q", g=G) for v in (qf, qrest)]
                link(V.tensor_copy(q1, f))
                link(V.tensor_tensor(out=r, in0=f, in1=q1, op=ALU.subtract))
                link(V.tensor_copy(q2, r))
                V.tensor_tensor(out=q3, in0=r, in1=q2, op=ALU.subtract).then_inc(s_qp, 1)
                for s, b, q in ((1, 0, q1), (2, 0, q1), (2, 1, q2), (3, 0, q2)):
                    V.tensor_copy(qstage[:, s, :, b, :], q).then_inc(s_qp, 1)

            def take_low(t, i, k):
                dve.wait_ge(s_ch, 2 * t + k + 1)
                nc.vector.tensor_tensor(out=ctxT_lo[i][:, k, :], in0=psTf[:, 0:TW], in1=ctxT_hi[i][:, k, :],
                                        op=ALU.subtract).then_inc(s_ct, 1)

            def key_tile(t, i, more, between=None):
                if more:
                    take_low(t + 1, 1 - i, 0)
                for g in range(G):
                    if more and g == TURN_G:
                        take_low(t + 1, 1 - i, 1)
                    if g == TURN_G and between:
                        between()
                    u = G * t + g
                    dve.wait_ge(s_k1, u + 1)
                    if not (isinstance(t, int) and u < 2):
                        dve.wait_ge(s_k3, u - 1)
                    nc.vector.scalar_tensor_tensor(
                        out=rest[g % 2].rearrange("p (a n) -> p a n", a=2), in0=psA[g % 2][:, :, 0:HW],
                        scalar=bk[:, g:g + 1], in1=part1[g].rearrange("p (a n) -> p a n", a=2),
                        op0=ALU.add, op1=ALU.subtract).then_inc(s_r, 1)
                    for c in range(2 * g, min(2 * g + 2, TC)):
                        w = TC * t + c
                        dve.wait_ge(s_vm, w + 1 + TC)
                        if c == 0 and not (isinstance(t, int) and t < 2):
                            dve.wait_ge(s_vw[i], 8 * (t - i))
                        nc.vector.tensor_tensor(out=vtile[i][:, :, c, 0:DH],
                                                in0=(psO, psM)[c % 2][:, 0:D].rearrange("p (h d) -> p h d", h=H),
                                                in1=bv_bc.rearrange("p (h d) -> p h d", h=H), op=ALU.add)\
                            .then_inc(s_v, 1)

            take_low(0, 0, 0)
            dve.wait_ge(s_wh, 1)
            nc.vector.tensor_tensor(out=wkv_lo, in0=wkv, in1=wkv_hi, op=ALU.subtract).then_inc(s_ws, 1)
            take_low(0, 0, 1)
            query_variance()
            make_select()
            dve.wait_ge(s_one, 3)
            dve.wait_ge(s_bkv, 32)
            query_norm()
            key_tile(0, 0, True)
            key_tile(1, 1, True, take_queries)
            query_parts()
            with dve.Fori(1, NT // 2 - 1) as i:
                for j in range(2):
                    key_tile(2 * i + j, j, True)
            key_tile(NT - 2, 0, True)
            key_tile(NT - 1, 1, False)

            def mask_first(hB, par, t):
                dve.wait_ge(s_exp, hB * NT + t + 1)
                n = slot(par, t)
                for lo, hi, done in ((0, C0 * P, s_msf), (C0 * P, TW, s_msk)):
                    nc.vector.scalar_tensor_tensor(
                        out=probs[:, n, lo:hi], in0=scores2[:, par, t * TW + lo:t * TW + hi],
                        scalar=thr[:, par:par + 1], in1=probs[:, n, lo:hi], op0=ALU.is_ge,
                        op1=ALU.mult).then_inc(done, 1)

            def mask_pair(hB, par, t):
                n = slot(par, t)
                dve.wait_ge(s_exp, hB * NT + t + 2)
                both = probs[:, n:n + 2, :].rearrange("p a n -> p (a n)")
                nc.vector.scalar_tensor_tensor(out=both, in0=scores2[:, par, t * TW:(t + 2) * TW],
                                               scalar=thr[:, par:par + 1], in1=both, op0=ALU.is_ge,
                                               op1=ALU.mult).then_inc(s_msk, 2)

            def take_candidates(hA, par, first, count):
                for i in range(first, first + count):
                    if i == first or i % NSUB == 0:
                        dve.wait_ge(s_cp, hA * NT + i // NSUB + 1)
                        dve.nop(nofuse=True)
                    nc.vector.max(cand[:, par, 8 * i:8 * i + 8],
                                  scores2[:, par, i * SUB:(i + 1) * SUB]).then_inc(s_max, 1)

            def threshold_steps(hT, par):
                c = cand[:, par, :]
                step = [0]

                def done():
                    dve.wait_ge(s_lk, hT * LINKS + step[0])
                    dve.nop(nofuse=True)

                def count(ins):
                    step[0] += 1
                    ins.then_inc(s_lk, 1)

                def bound():
                    dve.wait_ge(s_max, (hT + 1) * NT * NSUB)
                    count(nc.vector.tensor_reduce(flag[:, 1:2], c.rearrange("p (s e) -> p s e", e=8)[:, :, 7:8]
                                                  .rearrange("p s e -> p (s e)"), AX.X, ALU.max))

                def largest(r):
                    done()
                    count(nc.vector.max(top[:, 8 * r:8 * r + 8], c))

                def remove(r):
                    done()
                    count(nc.vector.match_replace(c, top[:, 8 * r:8 * r + 8], c, NEG))

                def raise_flag():
                    dve.wait_ge(s_lk, hT * LINKS + step[0])
                    nc.vector.tensor_tensor(out=flag[:, 0:1], in0=flag[:, 1:2], in1=top[:, TOPK - 1:TOPK],
                                            op=ALU.is_ge).then_inc(s_fl, 1)

                def read_flag():
                    dve.wait_ge(s_fs, hT + 1)
                    nc.vector.tensor_copy(flag_i[:, :], psH[par][0:1, 2 * P:2 * P + 1]).then_inc(s_fi, 1)

                def finish():
                    dve.wait_ge(s_fi, hT + 1)
                    dve.nop(nofuse=True)
                    flagged = dve.value_load(flag_i[0:1, 0:1], min_val=0, max_val=P)
                    with dve.If(flagged > 0):
                        general_threshold(par)
                    pcol = pos[:, hT:hT + 1] if isinstance(hT, int) else pos[:, bass.ds(hT, 1)]
                    count(nc.vector.tensor_copy(thr[:, par:par + 1], top[:, TOPK - 1:TOPK]))
                    count(nc.vector.tensor_tensor(out=rowmax[:, 0:1], in0=top[:, 0:1], in1=pcol, op=ALU.add))
                    dve.wait_ge(s_lk, hT * LINKS + step[0])
                    assert step[0] == LINKS - 1, step[0]
                    nc.vector.tensor_tensor(out=nbias[:, par:par + 1], in0=pcol, in1=rowmax[:, 0:1],
                                            op=ALU.subtract).then_inc(s_lk, 1)
                    dve.wait_ge(s_lk, (hT + 1) * LINKS)
                    dve.sem_inc(s_thr, 1)

                steps = [bound]
                for r in range(TOPK // 8):
                    steps.append(lambda r=r: largest(r))
                    if r + 1 < TOPK // 8:
                        steps.append(lambda r=r: remove(r))
                steps.append(raise_flag)
                assert len(steps) == FLAG_T
                return steps, read_flag, finish

            def general_threshold(par):
                cnt = [0]

                def chain(ins):
                    cnt[0] += 1
                    ins.then_inc(s_gen, 1)
                    dve.wait_ge(s_gen, cnt[0])

                def fold(src):
                    chain(nc.vector.tensor_copy(merge[:, TOPK:TOPK + SUB], src))
                    for r in range(TOPK // 8):
                        chain(nc.vector.max(top[:, 8 * r:8 * r + 8], merge[:, :]))
                        chain(nc.vector.match_replace(merge[:, :], top[:, 8 * r:8 * r + 8], merge[:, :], NEG))
                    chain(nc.vector.tensor_copy(merge[:, 0:TOPK], top[:, :]))
                    dve.sem_clear(s_gen)
                    cnt[0] = 0

                chain(nc.vector.memset(merge[:, 0:TOPK], NEG))
                dve.sem_clear(s_gen)
                cnt[0] = 0
                with dve.Fori(0, NT * NSUB) as i:
                    fold(scores2[:, par, bass.ds(i * SUB, SUB)])

            def take_output(hO, par):
                dve.wait_ge(s_pv, hO * NT + 2)
                dst = outT[:, hO, :] if isinstance(hO, int) else \
                    outT[:, bass.ds(hO, 1), :].rearrange("p o q -> p (o q)")
                nc.vector.tensor_copy(dst, psH[par][:, 0:P]).then_inc(s_oev, 1)

            def head(hB, hA, hT, par):
                plan = (0, 4, 3, 4, 3, 4, 3, 4, 3, 5, 4, 5, 4, 6) if hB is not None else (0,) + (NSUB,) * (NT - 1)
                assert sum(plan) == (NT - 1) * NSUB
                steps, read_flag, finish = threshold_steps(hT, 1 - par) if hT is not None else ([], None, None)
                for t in range(NT):
                    if hB is not None:
                        if hA is None:
                            mask_first(hB, par, t)
                        elif t % 2 == 0:
                            mask_pair(hB, par, t)
                        if t == 1:
                            take_output(hB, 1 - par)
                    if t > 0 and hA is not None:
                        take_candidates(hA, par, sum(plan[1:t]), plan[t])
                    elif t == 0 and hT is not None:
                        take_candidates(hT, 1 - par, (NT - 1) * NSUB, NSUB)
                    if t < len(steps):
                        steps[t]()
                    if hT is not None and t == FLAG_T + 1:
                        read_flag()
                    if hT is not None and t == FLAG_T + 2:
                        finish()

            head(None, 0, None, 0)
            head(None, 1, 0, 1)
            with dve.Fori(0, H // 2 - 1) as i:
                for par in range(2):
                    head(2 * i + par, 2 * i + par + 2, 2 * i + par + 1, par)
            head(H - 2, None, H - 1, 0)
            head(H - 1, None, None, 1)
            take_output(H, 1)
            vector_tail(dve)


def kernel(**inputs):
    import numpy as _np
    import concourse.bacc as _bacc
    from concourse import mybir as _mybir
    from concourse.bass_utils import run_bass_kernel_spmd as _run

    nc = _bacc.Bacc("TRN2", target_bir_lowering=False, num_devices=1)
    arrays, handles = {}, {}
    for name, value in inputs.items():
        v = _np.ascontiguousarray(value)
        if v.ndim == 0:
            v = v.reshape(1)
        arrays[f"in_{name}"] = v
        handles[name] = nc.dram_tensor(f"in_{name}", v.shape, _mybir.dt.from_np(v.dtype), kind="ExternalInput").ap()
    out = nc.dram_tensor("out_0", (1, P, D), _mybir.dt.float32, kind="ExternalOutput").ap()
    perceiver_block(nc, handles, out)
    r = _run(nc, [arrays], core_ids=[0])
    return r.results[0]["out_0"]
```
